# Optimizing a Trainium2 kernel written in Bass

```python
import numpy as np
import jax
import jax.numpy as jnp

def _softmax(x, axis=-1):
    return jax.nn.softmax(x, axis=axis)

def _gelu(x):
    return jax.nn.gelu(x, approximate=True)

def _silu(x):
    return jax.nn.silu(x)

def _sigmoid(x):
    return jax.nn.sigmoid(x)

def _layernorm(x, axis=-1, eps=1e-05):
    m = jnp.mean(x, axis=axis, keepdims=True)
    v = jnp.var(x, axis=axis, keepdims=True)
    return (x - m) / jnp.sqrt(v + eps)

def _scatter_add(tgt, idx, src, axis=0):
    return tgt.at[idx].add(src)

def _segment_sum(src, seg, n):
    return jax.ops.segment_sum(src, seg, n)
kernel_name = 'mk_macaron_d1_jaxref_r4_a535d3'

def setup_inputs(seed: int=0):
    np.random.seed(seed)
    _w = jnp.asarray

    def _L0_attn_setup():
        import jax, jax.numpy as jnp
        import numpy as np
        import math
        D_MODEL = 256
        NUM_HEADS = 16
        D_HEAD = D_MODEL // NUM_HEADS
        BATCH = 4
        SEQ = 512

        def _trunc_normal(key, shape, sd):
            return sd * jax.random.truncated_normal(key, -3.0, 3.0, shape, dtype=jnp.float32)
        key = jax.random.key(seed)
        kx, kq, kk, kv, ko = jax.random.split(key, 5)
        sd = (2.0 / (NUM_HEADS * D_HEAD + D_MODEL)) ** 0.5
        x = jax.random.normal(kx, (BATCH, SEQ, D_MODEL), dtype=jnp.float32)
        WQ = _trunc_normal(kq, (NUM_HEADS, D_HEAD, D_MODEL), sd)
        WK = _trunc_normal(kk, (NUM_HEADS, D_HEAD, D_MODEL), sd)
        WV = _trunc_normal(kv, (NUM_HEADS, D_HEAD, D_MODEL), sd)
        WO = _trunc_normal(ko, (NUM_HEADS, D_MODEL, D_HEAD), sd)
        return {'x': x, 'WQ': WQ, 'WK': WK, 'WV': WV, 'WO': WO}
    _L0_attn_in = _L0_attn_setup()

    def _L0_ffn_setup():
        import jax, jax.numpy as jnp
        import numpy as np
        D_MODEL = 256
        EXPANSION = 4
        D_HIDDEN = D_MODEL * EXPANSION
        NUM_STAGES = int(np.log2(D_HIDDEN))

        def butterfly(y, weights, dim):
            lead = y.shape[:-1]
            for stage in range(weights.shape[0]):
                s = 2 ** stage
                nb = dim // (2 * s)
                yr = y.reshape(*lead, nb, 2, s)
                a = yr[..., 0, :]
                b = yr[..., 1, :]
                w = weights[stage].reshape(nb, s, 2, 2)
                na = w[..., 0, 0] * a + w[..., 0, 1] * b
                nb2 = w[..., 1, 0] * a + w[..., 1, 1] * b
                y = jnp.stack([na, nb2], axis=-2).reshape(*lead, dim)
            return y
        key = jax.random.key(seed)
        ks = jax.random.split(key, 6)
        B, S = (4, 512)
        x = jax.random.normal(ks[0], (B, S, D_MODEL), jnp.float32)
        W_exp = jax.random.normal(ks[1], (D_MODEL, D_HIDDEN), jnp.float32) * 0.02
        b_exp = jnp.zeros((D_HIDDEN,), jnp.float32)
        up_weights = jax.random.normal(ks[2], (NUM_STAGES, D_HIDDEN // 2, 2, 2), jnp.float32) * 0.02
        up_bias = jnp.zeros((D_HIDDEN,), jnp.float32)
        down_weights = jax.random.normal(ks[3], (NUM_STAGES, D_HIDDEN // 2, 2, 2), jnp.float32) * 0.02
        W_con = jax.random.normal(ks[4], (D_HIDDEN, D_MODEL), jnp.float32) * 0.02
        b_con = jnp.zeros((D_MODEL,), jnp.float32)
        down_bias = jnp.zeros((D_MODEL,), jnp.float32)
        return dict(x=x, W_exp=W_exp, b_exp=b_exp, up_weights=up_weights, up_bias=up_bias, down_weights=down_weights, W_con=W_con, b_con=b_con, down_bias=down_bias)
    _L0_ffn_in = _L0_ffn_setup()
    _d = {'L0_attn_x': _L0_attn_in['x'], 'L0_attn_WQ': _L0_attn_in['WQ'], 'L0_attn_WK': _L0_attn_in['WK'], 'L0_attn_WV': _L0_attn_in['WV'], 'L0_attn_WO': _L0_attn_in['WO'], 'L0_ffn_W_exp': _L0_ffn_in['W_exp'], 'L0_ffn_b_exp': _L0_ffn_in['b_exp'], 'L0_ffn_up_weights': _L0_ffn_in['up_weights'], 'L0_ffn_up_bias': _L0_ffn_in['up_bias'], 'L0_ffn_down_weights': _L0_ffn_in['down_weights'], 'L0_ffn_W_con': _L0_ffn_in['W_con'], 'L0_ffn_b_con': _L0_ffn_in['b_con'], 'L0_ffn_down_bias': _L0_ffn_in['down_bias']}
    _x0 = _d['L0_attn_x']
    _d['L0_attn_x'] = jax.random.normal(jax.random.fold_in(jax.random.key(seed), 1), (1, 4096, 256), dtype=_x0.dtype)
    del _x0
    return _d

def reference(L0_attn_x, L0_attn_WQ, L0_attn_WK, L0_attn_WV, L0_attn_WO, L0_ffn_W_exp, L0_ffn_b_exp, L0_ffn_up_weights, L0_ffn_up_bias, L0_ffn_down_weights, L0_ffn_W_con, L0_ffn_b_con, L0_ffn_down_bias):

    def _L0_attn_ref(x, WQ, WK, WV, WO):
        import jax, jax.numpy as jnp
        import numpy as np
        import math
        D_MODEL = 256
        NUM_HEADS = 16
        D_HEAD = D_MODEL // NUM_HEADS
        BATCH = 4
        SEQ = 512

        def _trunc_normal(key, shape, sd):
            return sd * jax.random.truncated_normal(key, -3.0, 3.0, shape, dtype=jnp.float32)
        Q = jnp.einsum('bsd,hkd->bhsk', x, WQ)
        K = jnp.einsum('bsd,hkd->bhsk', x, WK)
        V = jnp.einsum('bsd,hkd->bhsk', x, WV)
        d_k = Q.shape[-1]
        scores = jnp.einsum('bhqd,bhkd->bhqk', Q, K) / math.sqrt(d_k)
        seq_len = x.shape[-2]
        causal = jnp.tril(jnp.ones((seq_len, seq_len), dtype=bool))
        scores = jnp.where(causal, scores, -jnp.inf)
        probs = jax.nn.softmax(scores, axis=-1)
        attn = jnp.einsum('bhqk,bhkv->bhqv', probs, V)
        return jnp.einsum('bhsv,hdv->bsd', attn, WO)

    def _L0_ffn_ref(x, W_exp, b_exp, up_weights, up_bias, down_weights, W_con, b_con, down_bias):
        import jax, jax.numpy as jnp
        import numpy as np
        D_MODEL = 256
        EXPANSION = 4
        D_HIDDEN = D_MODEL * EXPANSION
        NUM_STAGES = int(np.log2(D_HIDDEN))

        def butterfly(y, weights, dim):
            lead = y.shape[:-1]
            for stage in range(weights.shape[0]):
                s = 2 ** stage
                nb = dim // (2 * s)
                yr = y.reshape(*lead, nb, 2, s)
                a = yr[..., 0, :]
                b = yr[..., 1, :]
                w = weights[stage].reshape(nb, s, 2, 2)
                na = w[..., 0, 0] * a + w[..., 0, 1] * b
                nb2 = w[..., 1, 0] * a + w[..., 1, 1] * b
                y = jnp.stack([na, nb2], axis=-2).reshape(*lead, dim)
            return y
        h = jnp.einsum('bsd,dh->bsh', x, W_exp) + b_exp
        h = butterfly(h, up_weights, D_HIDDEN)
        h = jax.nn.gelu(h + up_bias, approximate=False)
        h = butterfly(h, down_weights, D_HIDDEN)
        y = jnp.einsum('bsh,hd->bsd', h, W_con) + b_con
        return y + down_bias
    x = L0_attn_x
    x = x + 0.5 * _L0_ffn_ref(_layernorm(x, axis=-1), L0_ffn_W_exp, L0_ffn_b_exp, L0_ffn_up_weights, L0_ffn_up_bias, L0_ffn_down_weights, L0_ffn_W_con, L0_ffn_b_con, L0_ffn_down_bias)
    x = x + _L0_attn_ref(_layernorm(x, axis=-1), L0_attn_WQ, L0_attn_WK, L0_attn_WV, L0_attn_WO)
    x = x + 0.5 * _L0_ffn_ref(_layernorm(x, axis=-1), L0_ffn_W_exp, L0_ffn_b_exp, L0_ffn_up_weights, L0_ffn_up_bias, L0_ffn_down_weights, L0_ffn_W_con, L0_ffn_b_con, L0_ffn_down_bias)
    return x

_drawn_inputs = setup_inputs


def setup_inputs(seed=0):
    import zlib

    import numpy as np

    out = dict(_drawn_inputs(seed))
    spreads = {'L0_ffn_b_exp': (0.0, 0.1),
     'L0_ffn_up_bias': (0.0, 0.1),
     'L0_ffn_b_con': (0.0, 0.1),
     'L0_ffn_down_bias': (0.0, 0.1)}
    factors = {}
    for name, (base, spread) in spreads.items():
        noise = np.random.default_rng([zlib.crc32(name.encode()), seed]).standard_normal(out[name].shape)
        drawn = base * np.exp(spread * noise) if base else spread * noise
        out[name] = jnp.asarray(drawn.astype(out[name].dtype))
    for name, factor in factors.items():
        out[name] = (out[name] * factor).astype(out[name].dtype)
    return out
```

```python
import concourse.bass as bass
from concourse import mybir
from contextlib import ExitStack

f32 = mybir.dt.float32
bf16 = mybir.dt.bfloat16
ALU = mybir.AluOpType
ACT = mybir.ActivationFunctionType
AX = mybir.AxisListType

S, D, H, DH = 4096, 256, 16, 16
HID, STAGES = 1024, 10
P = 128
TILE = 512
NT = S // TILE
NB = S // P
BT = TILE // P
DK = D // P
HB = HID // P
INNER = 7
DV = DH + 1
PARTS = 3
GROUPS = 6
SC = GROUPS * DH
SM = SC + PARTS
EPS = 1e-5
CH = [(j, c) for j in range(NT - 1, -1, -1) for c in range(j, -1, -1)]
NCH = len(CH)
LAST = {j: max(n for n, (a, _) in enumerate(CH) if a == j) for j in range(NT)}
NMX = NCH * BT
SLICE = 6 * 16
TB_AT, TA_AT = 2, 28


def w_offset(s):
    return 32 * (2 ** s - 1)


W_LEN = w_offset(INNER)
INNER_DMAS = sum(min(HB, P // 2 ** (s + 1)) for s in range(INNER))


def program(nc, x, w_exp_t, up_w, up_b, down_w, w_con, b_con, down_b, wq, wk, wv, wo, out):
    ctx = ExitStack()
    with ctx:
        def sb(name, shape, dt=f32):
            return ctx.enter_context(nc.sbuf_tensor(name, shape, dt))

        def sem(name):
            return ctx.enter_context(nc.semaphore(name))

        X = sb("X", [P, NB, D])
        OA = sb("OA", [P, NB, D])
        V = sb("V", [P, NB, H, DV])
        QK = sb("QK", [P, 4 * S // 2])
        PB = [sb(f"PB{i}", [P, 2, TILE]) for i in range(2)]
        VH = sb("VH", [P, NB, DV])
        MU = sb("MU", [P, DK, HID])
        MD = sb("MD", [P, HB, D])
        WQ, WK, WV, WO = (sb(n, [P, DK, D]) for n in ("WQ", "WK", "WV", "WO"))
        XN = sb("XN", [P, BT, D])
        XT = sb("XT", [P, DK, TILE])
        G = sb("G", [P, HB, TILE])
        SP3 = [sb(f"SP{i}", [P, PARTS, TILE], bf16) for i in range(2)]
        REST = [sb(f"REST{i}", [P, TILE]) for i in range(2)]
        MASK = sb("MASK", [P, TILE + 3 * P], bf16)
        ident = sb("ident", [P, P])
        identb = sb("identb", [P, P], bf16)
        beta = sb("beta", [P, INNER])
        nbeta = sb("nbeta", [P, INNER])
        DU = sb("DU", [P, 3, 4, 4])
        DD = sb("DD", [P, 3, 4, 4])
        UB = sb("UB", [P, HB])
        GB = sb("GB", [P, HB])
        OB = sb("OB", [P, D])
        OB2 = REST[0][:, 0:D]
        BNS = sb("BNS", [P, NB, 6])
        LN = sb("LN", [P, 4, NB])
        MEAN = sb("MEAN", [P, NB])
        RSTD = sb("RSTD", [P, NB])
        MXP = sb("MXP", [P, NB, NT])
        NEGM = sb("NEGM", [P, 3, NB // 2])
        MP = sb("MP", [P, 2, PARTS, NB // 2], bf16)
        MROW = [sb(f"MROW{i}", [PARTS * NB // 2, P], bf16) for i in range(2)]
        RC = sb("RC", [P, BT])
        PS = ctx.enter_context(nc.psum_tensor("PS", [P, 8 * 512], f32))

        def bank(b, n=512):
            return PS[:, b * 512:b * 512 + n]

        def qk(i):
            return QK[:, i * (S // 2):(i + 1) * (S // 2)].bitcast(bf16)

        CK, CQ, NK, NQ = (qk(i) for i in range(4))
        oa = OA[:, :, :].rearrange("p a b -> p (a b)")
        vv = V[:, :, :, :].rearrange("p a b c -> p (a b c)")
        g_ = G[:, :, :].rearrange("p a b -> p (a b)")

        def fold_scratch(t):
            o = W_LEN
            return dict(w=t[:, 0:o], a=[t[:, o:o + 1024], t[:, o + 1024:o + 2048]],
                        xa=t[:, o + 2048:o + 2560], xb=t[:, o + 2560:o + 3072], t=t[:, o + 3072:o + 4096])

        FU, FD = fold_scratch(oa), fold_scratch(vv)
        BW = D + 1
        WE = g_[:, 0:HB * BW].rearrange("p (b d) -> p b d", b=HB)
        WC = PB[0][:, :, :].rearrange("p a b -> p (a b)"), PB[1][:, :, :].rearrange("p a b -> p (a b)")
        T0 = QK[:, 0:HB * BW].rearrange("p (b d) -> p b d", b=HB)
        T1 = QK[:, HB * BW:2 * HB * BW].rearrange("p (b d) -> p b d", b=HB)
        TT = QK[:, 2 * HB * BW:3 * HB * BW].rearrange("p (b d) -> p b d", b=HB)
        AT = g_[:, 2560:2560 + 1024]

        def wc_block(b):
            return WC[b // 4][:, (b % 4) * D:(b % 4 + 1) * D]

        scratch = {n: nc.dram_tensor(f"{n}_parts", [PARTS, H * DH, S], bf16).ap() for n in "qk"}

        const_rdy, beta_rdy, dve_seq, pool_seq = sem("const_rdy"), sem("beta_rdy"), sem("dve_seq"), sem("pool_seq")
        in_up, in_down, in_we, in_wc, in_d, in_proj, in_bias = (
            sem(n) for n in ("in_up", "in_down", "in_we", "in_wc", "in_d", "in_proj", "in_bias"))
        x_in = [sem(f"x_in{t}") for t in range(NT)]
        a_up, a_down = sem("a_up"), sem("a_down")
        fold_ps, fold_ev, mix_a, mix_v, mu_ps, mu_ev = (
            sem(n) for n in ("fold_ps", "fold_ev", "mix_a", "mix_v", "mu_ps", "mu_ev"))
        at_ps, at_ev, md_ps, md_ev, gb_rdy, ob_rdy = (
            sem(n) for n in ("at_ps", "at_ev", "md_ps", "md_ev", "gb_rdy", "ob_rdy"))
        bns_done, ln_step, var_rdy, std_rdy = sem("bns_done"), sem("ln_step"), sem("var_rdy"), sem("std_rdy")
        xn_rdy, tr_ps, xt_rdy, xb_rdy = sem("xn_rdy"), sem("tr_ps"), sem("xt_rdy"), sem("xb_rdy")
        h_ps, gelu_done, y_ps, y_ev = sem("h_ps"), sem("gelu_done"), sem("y_ps"), sem("y_ev")
        qk_ps, hi_done, rest_done, mid_done, parts_done = (
            sem(n) for n in ("qk_ps", "hi_done", "rest_done", "mid_done", "parts_done"))
        parts_out = [sem(f"parts_out{i}") for i in range(2)]
        v_ps, v_ev = sem("v_ps"), sem("v_ev")
        att_init = sem("att_init")
        ld_cur = [sem(f"ld_cur{t}") for t in range(NT)]
        ld_nxt = [sem(f"ld_nxt{t}") for t in range(NT)]
        m_ld = [sem("m_ld0"), sem("m_ld1")]
        st_ps = [sem("st_ps0"), sem("st_ps1")]
        exp_done = [sem("exp_done0"), sem("exp_done1")]
        masked = [sem("masked0"), sem("masked1")]
        pv_done = [sem("pv_done0"), sem("pv_done1")]
        vh_rdy, mx_ps, mx_red, m_step, m_rdy, mt_ps, mt_ev = (
            sem(n) for n in ("vh_rdy", "mx_ps", "mx_red", "m_step", "m_rdy", "mt_ps", "mt_ev"))
        o_rc, o_ev, out_done = sem("o_rc"), sem("o_ev"), sem("out_done")
        passed = [sem(f"passed_{e}") for e in ("pool", "dve", "pe", "sp")]
        FREE_Y, FREE_H, FREE_QK, FREE_REST, FREE_V, FREE_MX, FREE_O = 2, 4, 4, 2, 2, 2, 2

        x_v = x.rearrange("(t b p) d -> t p b d", p=P, b=BT)
        out_v = out.rearrange("(t b p) d -> t p b d", p=P, b=BT)

        def tile_blocks(t):
            return bass.ds(t * BT, BT) if not isinstance(t, int) else slice(t * BT, (t + 1) * BT)

        def block_at(t, b):
            return bass.ds(t * BT + b, 1) if not isinstance(t, int) else slice(t * BT + b, t * BT + b + 1)

        def inner_product(eng, F, link):
            cur = F["a"][1]
            for s in range(INNER):
                n = 2 ** s
                nxt = F["a"][s % 2]
                o = w_offset(s)
                w = F["w"][:, o:o + HB * n * 4].rearrange("p (b c o e) -> p b o c e", b=HB, c=n, o=2)
                xa, xb = F["xa"][:, 0:HB * n], F["xb"][:, 0:HB * n]
                tmp = F["t"][:, 0:HB * 2 * n].rearrange("p (b o c) -> p b o c", b=HB, o=2)
                new = nxt[:, 0:HB * 2 * n].rearrange("p (b o c) -> p b o c", b=HB, o=2)

                def over_o(t):
                    return t.rearrange("p (b c) -> p b c", b=HB).unsqueeze(2).to_broadcast([P, HB, 2, n])

                eng.tensor_scalar(xa, cur[:, 0:HB * n], nbeta[:, s:s + 1], None, ALU.mult)
                link(eng.tensor_scalar(xb, cur[:, 0:HB * n], beta[:, s:s + 1], None, ALU.mult))
                eng.tensor_tensor(new, w[:, :, :, :, 0], over_o(xa), ALU.mult)
                link(eng.tensor_tensor(tmp, w[:, :, :, :, 1], over_o(xb), ALU.mult))
                link(eng.tensor_tensor(new, new, tmp, ALU.add))
                cur = nxt

        A_FINAL = (INNER - 1) % 2

        def mix_steps(down):
            order = (9, 8, 7) if down else (7, 8, 9)
            wt = DD if down else DU
            for k, s in enumerate(order):
                t = 2 ** (s - INNER)
                for b in range(HB):
                    bit = (b // t) & 1
                    pb = (b // (2 * t)) * t + b % t
                    ia, ib = (bit, 2 + bit) if down else (2 * bit, 2 * bit + 1)
                    yield k, b, b & ~t, b | t, wt[:, s - INNER, pb, ia:ia + 1], wt[:, s - INNER, pb, ib:ib + 1]

        def mix_src(down, k, b):
            if k == 0 and down:
                return wc_block(b)
            w = D if down else BW
            return (T0, T1)[k % 2][:, b, 0:w]

        def mix_dst(down, k, b):
            w = D if down else BW
            return (T1, T0)[k % 2][:, b, 0:w]

        block = ctx.enter_context(nc.Block())

        @block.sync
        def _(sp):
            for i in range(2):
                sp.sem_inc(parts_out[i], 16)

            def inner_weights(src, dst, s, sig):
                n = 2 ** s
                hi = P // (2 * n)
                o = w_offset(s)
                d = dst[:, o:o + HB * n * 4].rearrange("p (b c) -> p b c", b=HB)
                w = src[s].rearrange("(b h c) e -> h b (c e)", b=HB, h=hi)
                if hi <= HB:
                    for k in range(hi):
                        sp.dma_start(d[2 * n * k:2 * n * (k + 1)], w[k:k + 1].to_broadcast([2 * n, HB, n * 4])
                                     ).then_inc(sig, 16)
                else:
                    for b in range(HB):
                        sp.dma_start(d[:, b, :], w[:, b, :].unsqueeze(1).to_broadcast([hi, 2 * n, n * 4])
                                     ).then_inc(sig, 16)

            for s in range(INNER):
                inner_weights(up_w, FU["w"], s, in_up)
            sp.dma_start(WE[:, :, :], w_exp_t.rearrange("(b p) d -> p b d", p=P)).then_inc(in_we, 16)
            for w, d in ((up_w, DU), (down_w, DD)):
                sp.dma_start(d[:, :, :, :], w[INNER:STAGES].rearrange("s (g p) e -> p s g e", p=P)).then_inc(in_d, 16)
            sp.dma_start(UB[:, :], up_b).then_inc(in_d, 16)
            sp.dma_start(OB[:, :], b_con.rearrange("(o d) -> o d", o=1).to_broadcast([P, D])).then_inc(in_bias, 16)
            sp.dma_start(OB2[:, :], down_b.rearrange("(o d) -> o d", o=1).to_broadcast([P, D])).then_inc(in_bias, 16)
            for t in range(NT):
                sp.dma_start(X[:, t * BT:(t + 1) * BT, :], x_v[t]).then_inc(x_in[t], 16)
            for s in range(INNER):
                inner_weights(down_w, FD["w"], s, in_down)
            for i in range(2):
                sp.dma_start(WC[i].rearrange("p (b d) -> p b d", d=D),
                             w_con[i * 512:(i + 1) * 512, :].rearrange("(b p) d -> p b d", p=P)).then_inc(in_wc, 16)
            for d, w in ((WQ, wq), (WK, wk), (WV, wv), (WO, wo)):
                sp.dma_start(d[:, :, :], w.rearrange("(k p) n -> p k n", p=P)).then_inc(in_proj, 16)

            with sp.Fori(0, NT) as t:
                for w in range(4):
                    sp.wait_ge(parts_done, t * 4 + w + 1 + FREE_REST)
                    dst = scratch["q" if w < 2 else "k"][:, (w % 2) * P:(w % 2 + 1) * P, bass.ds(t * TILE, TILE)]
                    sp.dma_start(dst.rearrange("a p t -> p a t"), SP3[w % 2][:, :, :]).then_inc(parts_out[w % 2], 16)
            for i in range(2):
                sp.wait_ge(parts_out[i], 16 * (2 * NT + 1))
            sp.wait_ge(att_init, 1)

            def load_slice(kt, qt, h, j, sig):
                ts = slice(j * TILE, (j + 1) * TILE)
                hs = bass.ds(h * DH, DH) if not isinstance(h, int) else slice(h * DH, (h + 1) * DH)

                def part(name, p0, n, rep):
                    s = scratch[name][p0:p0 + n, hs, ts]
                    return s.to_broadcast([rep, DH, TILE]) if rep > 1 else s

                for dst, name, r0, p0, n, rep in (
                        (kt, "k", 0, 0, 3, 1), (kt, "k", 3, 0, 2, 1), (kt, "k", 5, 0, 1, 1),
                        (qt, "q", 0, 0, 1, 3), (qt, "q", 3, 1, 1, 2), (qt, "q", 5, 2, 1, 1)):
                    g = max(n, rep)
                    sp.dma_start(dst[r0 * DH:(r0 + g) * DH, ts], part(name, p0, n, rep)).then_inc(sig, 16)

            def load_m(i, g):
                sp.wait_ge(mt_ev, i + 1)
                half = NB // 2
                c0 = (1 - g) * (S // 2)
                for p in range(PARTS):
                    sp.dma_start(CQ[SC + p:SC + p + 1, c0:c0 + S // 2], MROW[g][p * half:(p + 1) * half, :]
                                 ).then_inc(m_ld[g], 16)

            for j in range(NT - 1, -1, -1):
                load_slice(NK, NQ, 0, j, ld_nxt[j])
            for j in range(NT - 1, -1, -1):
                load_slice(CK, CQ, 0, j, ld_cur[j])
            for j in range(NT - 1, -1, -1):
                sp.wait_ge(mx_ps, BT * LAST[j] + BT)
                load_slice(NK, NQ, 1, j, ld_nxt[j])
            load_m(0, 0)

            def head_loads(h, more):
                for j in range(NT - 1, -1, -1):
                    sp.wait_ge(st_ps[1], h * NCH + LAST[j] + 1)
                    sp.sem_inc(passed[3], 1)
                    load_slice(CK, CQ, h + 1, j, ld_cur[j])
                    if more:
                        sp.wait_ge(mx_ps, (h + 1) * NMX + BT * LAST[j] + BT)
                        sp.sem_inc(passed[3], 1)
                        load_slice(NK, NQ, h + 2, j, ld_nxt[j])
                    if j == NT - 1:
                        load_m(2 * h + 1, 1)
                    if j == 3:
                        load_m(2 * h + 2, 0)

            with sp.Fori(0, H - 2) as h:
                head_loads(h, True)
            head_loads(H - 2, False)
            load_m(2 * H - 1, 1)

            with sp.Fori(0, NT) as t:
                sp.wait_ge(y_ev, (t + 2 * NT) * BT + BT + FREE_Y)
                sp.dma_start(out.rearrange("(b p) d -> p b d", p=P)[:, bass.ds(t * BT, BT), :],
                             X[:, bass.ds(t * BT, BT), :]).then_inc(out_done, 16)
            sp.wait_ge(out_done, 16 * NT)
            for g in range(2):
                sp.wait_ge(m_ld[g], 48 * H)

        @block.gpsimd
        def _(pool):
            seq = [0]

            def link(ins):
                seq[0] += 1
                ins.then_inc(pool_seq, 1)
                pool.wait_ge(pool_seq, seq[0])

            link(nc.gpsimd.memset(ident[:, :], 0.0))
            nc.gpsimd.affine_select(out=ident[:, :], in_=ident[:, :], compare_op=ALU.not_equal, fill=1.0, base=0,
                                    pattern=[[-1, P]], channel_multiplier=1).then_inc(const_rdy, 1)
            link(nc.gpsimd.memset(MASK[:, :], 0.0))
            nc.gpsimd.affine_select(out=MASK[:, :], in_=MASK[:, :], compare_op=ALU.is_ge, fill=-1e30, base=3 * P,
                                    pattern=[[-1, TILE + 3 * P]], channel_multiplier=1).then_inc(const_rdy, 1)
            link(nc.gpsimd.memset(FD["a"][1][:, 0:HB], 1.0))
            pool.wait_ge(beta_rdy, 1)
            pool.wait_ge(in_down, 16 * INNER_DMAS)
            inner_product(nc.gpsimd, FD, link)
            pool.sem_inc(a_down, 1)
            pool.sem_inc(parts_done, FREE_REST)

            def add_bias(t, n):
                pool.wait_ge(xn_rdy, n + 1)
                nc.gpsimd.tensor_tensor(X[:, tile_blocks(t), :], X[:, tile_blocks(t), :],
                                        OB[:, :].unsqueeze(1).to_broadcast([P, BT, D]), ALU.add).then_inc(xb_rdy, 1)

            pool.wait_ge(ob_rdy, 1)
            with pool.Fori(0, NT) as t:
                add_bias(t, t)

            with pool.Fori(0, NT) as t:
                for w in range(4):
                    u = t * 4 + w
                    pool.wait_ge(rest_done, u + 1 + FREE_QK)
                    pool.sem_inc(passed[0], 1)
                    nc.gpsimd.tensor_copy(SP3[w % 2][:, 1, :], REST[w % 2][:, :]).then_inc(mid_done, 1)
                    pool.wait_ge(mid_done, u + 1)
                    nc.gpsimd.tensor_tensor(SP3[w % 2][:, 2, :], REST[w % 2][:, :], SP3[w % 2][:, 1, :],
                                            ALU.subtract).then_inc(parts_done, 1)

            def copy_v(h, j, done):
                pool.wait_ge(pv_done[1], done + 1)
                pool.sem_inc(passed[0], 1)
                hs = slice(h, h + 1) if isinstance(h, int) else bass.ds(h, 1)
                nc.gpsimd.tensor_copy(VH[:, j * BT:(j + 1) * BT, :],
                                      V[:, j * BT:(j + 1) * BT, hs, :].rearrange("p b o v -> p b (o v)")
                                      ).then_inc(vh_rdy, 1)

            def head_masks(h, more):
                for j in range(NT - 1, -1, -1):
                    n = CH.index((j, j))
                    for half in range(2):
                        pool.wait_ge(exp_done[half], h * NCH + n + 1)
                        pool.sem_inc(passed[0], 1)
                        for k in range(2):
                            c0 = (2 * half + k) * P
                            tri = PB[half][:, k, c0:c0 + P]
                            nc.gpsimd.affine_select(out=tri, in_=tri, compare_op=ALU.is_ge, fill=0.0, base=0,
                                                    pattern=[[1, P]], channel_multiplier=-1).then_inc(masked[half], 1)
                    if j == NT - 1:
                        copy_v(h, 0, h * NCH)
                    elif more:
                        copy_v(h + 1, j + 1, h * NCH + LAST[j + 1] + 1)

            pool.wait_ge(v_ev, NT * BT + FREE_V)
            for j in range(NT - 1, 0, -1):
                nc.gpsimd.tensor_copy(VH[:, j * BT:(j + 1) * BT, :],
                                      V[:, j * BT:(j + 1) * BT, 0, :]).then_inc(vh_rdy, 1)
            with pool.Fori(0, H - 1) as h:
                head_masks(h, True)
            head_masks(H - 1, False)

            with pool.Fori(0, NT) as t:
                add_bias(t, t + 3 * NT)

        @block.scalar
        def _(act):
            act.sem_inc(gelu_done, FREE_H)
            act.sem_inc(v_ev, FREE_V)
            for b in range(HB):
                act.wait_ge(fold_ps, b + 1)
                nc.scalar.activation(T0[:, b, :], bank(b, BW), ACT.Copy).then_inc(fold_ev, 1)
            act.wait_ge(in_d, 48)
            act.wait_ge(fold_ev, HB)

            def mix_a_side(down):
                for k, b, ia, ib, wa, wb in mix_steps(down):
                    if b == 0 and (k or down):
                        act.wait_ge(mix_v, HB * (k + 3 * down))
                    nc.scalar.activation(TT[:, b, 0:D if down else BW], mix_src(down, k, ia), ACT.Copy,
                                         scale=wa).then_inc(mix_a, 1)

            mix_a_side(0)
            for i in range(4):
                act.wait_ge(mu_ps, i + 1)
                nc.scalar.activation(MU[:, i // 2, (i % 2) * 512:(i % 2 + 1) * 512], bank(i), ACT.Copy
                                     ).then_inc(mu_ev, 1)
            act.wait_ge(in_wc, 32)
            mix_a_side(1)
            for i in range(2):
                act.wait_ge(at_ps, i + 1)
                nc.scalar.activation(AT[:, i * 512:(i + 1) * 512], bank(4 + i), ACT.Copy).then_inc(at_ev, 1)
            for i in range(4):
                act.wait_ge(md_ps, i + 1)
                nc.scalar.activation(MD[:, 2 * i:2 * i + 2, :].rearrange("p a b -> p (a b)"), bank(4 + i), ACT.Copy,
                                     scale=0.5).then_inc(md_ev, 1)

            def std(k):
                act.wait_ge(var_rdy, k + 1)
                nc.scalar.activation(LN[:, 3, :], LN[:, 2, :], ACT.Sqrt).then_inc(std_rdy, 1)

            def gelus(n, y):
                act.wait_ge(y_ps, y * BT + 1)
                for b in range(HB):
                    act.wait_ge(h_ps, n * HB + b + 1)
                    nc.scalar.activation(G[:, b, :], bank(2 + b % 4), ACT.Gelu, bias=GB[:, b:b + 1]
                                         ).then_inc(gelu_done, 1)

            std(0)
            act.wait_ge(gb_rdy, 1)
            act.wait_ge(md_ev, 4)
            with act.Fori(0, NT) as t:
                gelus(t, t)
            std(1)

            with act.Fori(0, NT) as t:
                for w in range(4):
                    act.wait_ge(parts_out[w % 2], (t * 2 + w // 2) * 16 + 16)
                    act.wait_ge(qk_ps, t * 4 + w + 1)
                    nc.scalar.activation(SP3[w % 2][:, 0, :], bank(2 + w), ACT.Copy).then_inc(hi_done, 1)
                for b in range(BT):
                    act.wait_ge(v_ps, t * BT + b + 1)
                    nc.scalar.activation(V[:, bass.ds(t * BT + b, 1), :, 0:DH].rearrange("p o h v -> p (o h) v"),
                                         bank(6 + b % 2, D).rearrange("p (h v) -> p h v", v=DH), ACT.Copy
                                         ).then_inc(v_ev, 1)

            def exps(h):
                for n, (j, c) in enumerate(CH):
                    for half in range(2):
                        q0 = 2 * P if (j == c and half) else 0
                        act.wait_ge(st_ps[half], h * NCH + n + 1)
                        act.wait_ge(pv_done[half], h * NCH + n + 1)
                        nc.scalar.activation(
                            PB[half][:, :, q0:TILE],
                            PS[:, half * 1024:half * 1024 + 1024].rearrange("p (k q) -> p k q", k=2)[:, :, q0:TILE],
                            ACT.Exp, scale=1.0 / DH ** 0.5).then_inc(exp_done[half], 1)

            with act.Fori(0, H) as h:
                exps(h)

            def o_rows(t):
                act.wait_ge(tr_ps, t + 2 * NT)
                nc.scalar.activation(XN[:, :, :], OA[:, tile_blocks(t), :], ACT.Copy).then_inc(xn_rdy, 1)

            act.wait_ge(o_ev, H * NT + FREE_O)
            with act.Fori(0, NT) as t:
                o_rows(t)
            std(2)
            with act.Fori(0, NT) as t:
                gelus(t + NT, t + 2 * NT)

        @block.vector
        def _(dve):
            seq = [0]

            def link(ins):
                seq[0] += 1
                ins.then_inc(dve_seq, 1)
                dve.wait_ge(dve_seq, seq[0])

            dve.sem_inc(y_ev, FREE_Y)
            dve.sem_inc(rest_done, FREE_QK)
            dve.sem_inc(mx_red, FREE_MX)
            dve.sem_inc(o_ev, FREE_O)
            nc.vector.memset(MXP[:, :, :], -3e38)
            nc.vector.memset(FU["a"][1][:, 0:HB], 1.0)
            dve.wait_ge(const_rdy, 1)
            nc.vector.tensor_copy(identb[:, :], ident[:, :])
            for s in range(INNER):
                v = ident[:, :].rearrange("p (h b l) -> p h b l", b=2, l=2 ** s)[:, :, 1, :]
                last = nc.vector.tensor_reduce(beta[:, s:s + 1], v, AX.XY, ALU.add)
            link(last)
            nc.vector.tensor_scalar(nbeta[:, :], beta[:, :], -1.0, 1.0, ALU.mult, ALU.add).then_inc(beta_rdy, 1)
            dve.wait_ge(beta_rdy, 1)
            dve.wait_ge(in_up, 16 * INNER_DMAS)
            inner_product(nc.vector, FU, link)
            dve.sem_inc(a_up, 1)

            def stats(t, b):
                nc.vector.bn_stats(BNS[:, block_at(t, b), :].rearrange("p o s -> p (o s)"),
                                   X[:, block_at(t, b), :].rearrange("p o d -> p (o d)")).then_inc(bns_done, 1)

            for t in range(NT):
                dve.wait_ge(x_in[t], 16)
                for b in range(BT):
                    stats(t, b)

            def finish_stats(k):
                def step(ins, n):
                    ins.then_inc(ln_step, 1)
                    dve.wait_ge(ln_step, 6 * k + n)
                me, mo = BNS[:, :, 1], BNS[:, :, 4]
                ve, vo = BNS[:, :, 2], BNS[:, :, 5]
                dve.wait_ge(bns_done, NB * (k + 1))
                nc.vector.tensor_tensor(LN[:, 0, :], me, mo, ALU.add)
                step(nc.vector.tensor_tensor(LN[:, 1, :], me, mo, ALU.subtract), 1)
                nc.vector.tensor_scalar(MEAN[:, :], LN[:, 0, :], 0.5, None, ALU.mult)
                step(nc.vector.tensor_tensor(LN[:, 2, :], LN[:, 1, :], LN[:, 1, :], ALU.mult), 2)
                step(nc.vector.tensor_tensor(LN[:, 0, :], ve, vo, ALU.add), 3)
                step(nc.vector.tensor_scalar(LN[:, 1, :], LN[:, 0, :], 1.0 / D, EPS, ALU.mult, ALU.add), 4)
                nc.vector.scalar_tensor_tensor(LN[:, 2, :], LN[:, 2, :], 0.25, LN[:, 1, :], ALU.mult, ALU.add
                                               ).then_inc(var_rdy, 1)
                dve.wait_ge(std_rdy, k + 1)
                step(nc.vector.reciprocal(RSTD[:, :], LN[:, 3, :]), 5)
                step(nc.vector.tensor_copy(LN[:, 0, :], RSTD[:, :]), 6)

            def mix_v_side(down):
                for i, (k, b, ia, ib, wa, wb) in enumerate(mix_steps(down)):
                    if b == 0 and (k or down):
                        dve.wait_ge(mix_v, HB * (k + 3 * down))
                    dve.wait_ge(mix_a, HB * 3 * down + i + 1)
                    nc.vector.scalar_tensor_tensor(mix_dst(down, k, b), mix_src(down, k, ib), wb,
                                                   TT[:, b, 0:D if down else BW], ALU.mult, ALU.add
                                                   ).then_inc(mix_v, 1)

            dve.wait_ge(in_d, 48)
            dve.wait_ge(fold_ev, HB)
            mix_v_side(0)
            dve.wait_ge(mix_v, 3 * HB)
            nc.vector.tensor_tensor(GB[:, :], T1[:, :, D], UB[:, :], ALU.add).then_inc(gb_rdy, 1)
            dve.wait_ge(in_bias, 32)
            link(nc.vector.tensor_tensor(OB[:, :], OB[:, :], OB2[:, :], ALU.add))
            nc.vector.tensor_scalar(OB[:, :], OB[:, :], 0.5, None, ALU.mult).then_inc(ob_rdy, 1)
            dve.wait_ge(mu_ps, 4)
            dve.wait_ge(gb_rdy, 1)
            mix_v_side(1)
            finish_stats(0)

            def normalize(t, n):
                if not (isinstance(n, int) and n == 0):
                    dve.wait_ge(tr_ps, n)
                for b in range(BT):
                    last = nc.vector.tensor_scalar(
                        XN[:, b, :], X[:, block_at(t, b), :].rearrange("p o d -> p (o d)"),
                        MEAN[:, block_at(t, b)], RSTD[:, block_at(t, b)], ALU.subtract, ALU.mult)
                last.then_inc(xn_rdy, 1)

            def take_transposed(n):
                dve.wait_ge(tr_ps, n + 1)
                for k in range(DK):
                    last = nc.vector.tensor_copy(XT[:, k, :], bank(k))
                last.then_inc(xt_rdy, 1)

            def residual(t, y, bias, with_stats):
                if bias is not None:
                    dve.wait_ge(xb_rdy, bias + 1)
                for b in range(BT):
                    dve.wait_ge(y_ps, y * BT + b + 2)
                    xb = X[:, block_at(t, b), :].rearrange("p o d -> p (o d)")
                    nc.vector.tensor_tensor(xb, bank(6 + b % 2, D), xb, ALU.add).then_inc(y_ev, 1)
                if with_stats:
                    for b in range(BT):
                        dve.wait_ge(y_ev, y * BT + b + 1 + FREE_Y)
                        stats(t, b)

            def ffn(n0, y0, bias0, with_stats):
                normalize(0, n0)
                take_transposed(n0)
                with dve.Fori(0, NT - 1) as t:
                    normalize(t + 1, t + n0 + 1)
                    take_transposed(t + n0 + 1)
                    residual(t, t + y0, t + bias0, with_stats)
                residual(NT - 1, NT - 1 + y0, NT - 1 + bias0, with_stats)

            ffn(0, 0, 0, True)
            nc.vector.memset(V[:, :, :, DH:DV], 1.0)
            dve.wait_ge(xn_rdy, NT)
            finish_stats(1)

            def rests(t):
                for w in range(4):
                    u = t * 4 + w
                    dve.wait_ge(hi_done, u + 1)
                    dve.wait_ge(parts_done, u + 1)
                    nc.vector.tensor_tensor(REST[w % 2][:, :], bank(2 + w), SP3[w % 2][:, 0, :], ALU.subtract
                                            ).then_inc(rest_done, 1)

            normalize(0, NT)
            take_transposed(NT)
            with dve.Fori(0, NT - 1) as t:
                rests(t)
                normalize(t + 1, t + NT + 1)
                take_transposed(t + NT + 1)
            rests(NT - 1)
            nc.vector.memset(CK[96:SM, :], 1.0).then_inc(att_init, 1)

            def maxima(g, n, pair):
                j, c = CH[n]
                for i in range(2):
                    qs = 2 * pair + i
                    item = n * BT + qs
                    dve.wait_ge(mx_ps, g * NMX + item + 1)
                    dst = MXP[:, BT * j + qs, c:c + 1]
                    if j == c:
                        w = (qs + 1) * P
                        s = bank(4 + qs % 2, w)
                        dve.sem_inc(passed[1], 1)
                        nc.vector.tensor_tensor_reduce(out=s, in0=s, in1=MASK[:, 3 * P - qs * P:3 * P - qs * P + w],
                                                       scale=1.0, scalar=-3e38, op0=ALU.add, op1=ALU.max,
                                                       accum_out=dst).then_inc(mx_red, 1)
                    else:
                        nc.vector.tensor_reduce(dst, bank(4 + qs % 2), AX.X, ALU.max).then_inc(mx_red, 1)

            def split_maxima(g, grp):
                i = 2 * g + grp
                nb = NB // 2
                r = [NEGM[:, k, :] for k in range(3)]
                mp = [MP[:, grp, k, :] for k in range(PARTS)]

                def step(ins, k):
                    ins.then_inc(m_step, 1)
                    dve.wait_ge(m_step, i * 5 + k)
                dve.wait_ge(mx_red, g * NMX + (LAST[4] + 1) * BT * (1 - grp) + NMX * grp + FREE_MX)
                step(nc.vector.tensor_reduce(r[0], MXP[:, (1 - grp) * nb:(2 - grp) * nb, :], AX.X, ALU.max,
                                             negate=True), 1)
                step(nc.vector.tensor_copy(mp[0], r[0]), 2)
                step(nc.vector.tensor_tensor(r[1], r[0], mp[0], ALU.subtract), 3)
                step(nc.vector.tensor_copy(mp[1], r[1]), 4)
                step(nc.vector.tensor_tensor(r[2], r[1], mp[1], ALU.subtract), 5)
                nc.vector.tensor_copy(mp[2], r[2]).then_inc(m_rdy, 1)

            def take_rows(i, grp):
                dve.wait_ge(mt_ps, i + 1)
                nc.vector.tensor_copy(MROW[grp][:, :], PS[0:PARTS * NB // 2, 6 * 512:6 * 512 + P // 2].bitcast(bf16)
                                      ).then_inc(mt_ev, 1)

            def take_o(h, j):
                q = h * NT + (NT - 1 - j)
                O = bank(6 + j % 2, BT * DV).rearrange("p (b v) -> p b v", v=DV)
                dve.wait_ge(pv_done[1], h * NCH + LAST[j] + 2)
                dve.wait_ge(o_ev, q + FREE_O)
                nc.vector.reciprocal(RC[:, :], O[:, :, DH]).then_inc(o_rc, 1)
                dve.wait_ge(o_rc, q + 1)
                hs = slice(h * DH, (h + 1) * DH) if isinstance(h, int) else bass.ds(h * DH, DH)
                nc.vector.tensor_tensor(OA[:, j * BT:(j + 1) * BT, hs], O[:, :, 0:DH],
                                        RC[:, :].unsqueeze(2).to_broadcast([P, BT, DH]), ALU.mult).then_inc(o_ev, 1)

            def head(h, more):
                for n, (j, c) in enumerate(CH):
                    if more:
                        maxima(h + 1, n, 0)
                    if n == LAST[j]:
                        take_o(h, j)
                    if more:
                        maxima(h + 1, n, 1)
                        if n == LAST[4]:
                            split_maxima(h + 1, 0)
                        if n == TA_AT:
                            take_rows(2 * h + 2, 0)
                    if n == TB_AT:
                        take_rows(2 * h + 1, 1)
                if more:
                    split_maxima(h + 1, 1)

            for n in range(NCH):
                maxima(0, n, 0)
                maxima(0, n, 1)
                if n == LAST[4]:
                    split_maxima(0, 0)
                if n == TA_AT:
                    take_rows(0, 0)
            split_maxima(0, 1)
            with dve.Fori(0, H - 1) as h:
                head(h, True)
            head(H - 1, False)

            take_transposed(2 * NT)
            with dve.Fori(0, NT - 1) as t:
                residual(t, t + NT, None, True)
                take_transposed(t + 2 * NT + 1)
            residual(NT - 1, 2 * NT - 1, None, True)
            finish_stats(2)
            ffn(3 * NT, 2 * NT, NT, False)

        @block.tensor
        def _(pe):
            mm = nc.tensor.matmul
            pe.sem_inc(y_ps, 1)
            pe.sem_inc(pv_done[0], 1)
            pe.sem_inc(pv_done[1], 1)
            pe.wait_ge(a_up, 1)
            pe.wait_ge(in_we, 16)
            AU, AD = FU["a"][A_FINAL], FD["a"][A_FINAL]
            for b in range(HB):
                mm(bank(b, BW), AU[:, b * P:(b + 1) * P], WE[:, b, :], start=True, stop=True).then_inc(fold_ps, 1)
            pe.wait_ge(fold_ev, HB)
            pe.wait_ge(mix_v, 3 * HB)
            for i in range(4):
                for k in range(4):
                    last = nc.tensor.transpose(PS[:, i * 512 + k * P:i * 512 + (k + 1) * P],
                                               T1[:, (i % 2) * 4 + k, (i // 2) * P:(i // 2 + 1) * P], ident[:, :])
                last.then_inc(mu_ps, 1)
            pe.wait_ge(a_down, 1)
            for i in range(2):
                for k in range(4):
                    b = 4 * i + k
                    last = nc.tensor.transpose(PS[:, (4 + i) * 512 + k * P:(4 + i) * 512 + (k + 1) * P],
                                               AD[:, b * P:(b + 1) * P], ident[:, :])
                last.then_inc(at_ps, 1)
            pe.wait_ge(at_ev, 2)
            pe.wait_ge(mix_v, 6 * HB)
            for i in range(4):
                for k in range(2):
                    b = 2 * i + k
                    last = mm(PS[:, (4 + i) * 512 + k * D:(4 + i) * 512 + (k + 1) * D], AT[:, b * P:(b + 1) * P],
                              T1[:, b, 0:D], start=True, stop=True)
                last.then_inc(md_ps, 1)

            def transposes(n):
                pe.wait_ge(xn_rdy, n + 1)
                if not (isinstance(n, int) and n == 0):
                    pe.wait_ge(xt_rdy, n)
                for k in range(DK):
                    for b in range(BT):
                        last = nc.tensor.transpose(PS[:, k * 512 + b * P:k * 512 + (b + 1) * P],
                                                   XN[:, b, k * P:(k + 1) * P], ident[:, :])
                last.then_inc(tr_ps, 1)

            def up(n, x):
                pe.wait_ge(xt_rdy, x + 1)
                for b in range(HB):
                    pe.wait_ge(gelu_done, n * HB + b + 1)
                    for k in range(DK):
                        last = mm(bank(2 + b % 4), MU[:, k, b * P:(b + 1) * P], XT[:, k, :],
                                  start=(k == 0), stop=(k == DK - 1))
                    last.then_inc(h_ps, 1)

            def y_out(y, lhs, rhs, nk):
                for b in range(BT):
                    pe.wait_ge(y_ev, y * BT + b + 1)
                    for k in range(nk):
                        last = mm(bank(6 + b % 2, D), lhs[:, k, b * P:(b + 1) * P], rhs[:, k, :],
                                  start=(k == 0), stop=(k == nk - 1))
                    last.then_inc(y_ps, 1)

            def down(n, y):
                pe.wait_ge(gelu_done, n * HB + HB + FREE_H)
                y_out(y, G, MD, HB)

            def ffn(n0, x0, y0):
                transposes(x0)
                with pe.Fori(0, NT - 1) as t:
                    up(t + n0, t + x0)
                    transposes(t + x0 + 1)
                    down(t + n0, t + y0)
                up(NT - 1 + n0, NT - 1 + x0)
                down(NT - 1 + n0, NT - 1 + y0)

            pe.wait_ge(mu_ev, 4)
            pe.wait_ge(md_ev, 4)
            ffn(0, 0, 0)

            pe.wait_ge(in_proj, 64)

            def project(t):
                pe.wait_ge(xt_rdy, t + NT + 1)
                for w in range(4):
                    pe.wait_ge(rest_done, t * 4 + w + 1)
                    for k in range(DK):
                        last = mm(bank(2 + w), (WQ if w < 2 else WK)[:, k, (w % 2) * P:(w % 2 + 1) * P], XT[:, k, :],
                                  start=(k == 0), stop=(k == DK - 1))
                    last.then_inc(qk_ps, 1)
                for b in range(BT):
                    pe.wait_ge(v_ev, t * BT + b + 1)
                    for k in range(DK):
                        last = mm(bank(6 + b % 2, D), XT[:, k, b * P:(b + 1) * P], WV[:, k, :],
                                  start=(k == 0), stop=(k == DK - 1))
                    last.then_inc(v_ps, 1)

            transposes(NT)
            with pe.Fori(0, NT - 1) as t:
                project(t)
                transposes(t + NT + 1)
            project(NT - 1)
            pe.wait_ge(rest_done, 4 * NT + FREE_QK)
            pe.wait_ge(v_ev, NT * BT + FREE_V)

            def scores(h, n, half):
                j, c = CH[n]
                if half == 0 and j == NT - 1:
                    pe.wait_ge(ld_cur[c], h * SLICE + SLICE)
                if half == 0 and n == 0:
                    pe.wait_ge(m_ld[0], h * 48 + 48)
                if half == 0 and n == LAST[4] + 1:
                    pe.wait_ge(m_ld[1], h * 48 + 48)
                q0 = 2 * P if (j == c and half) else 0
                for k in range(2):
                    kb = c * BT + 2 * half + k
                    last = mm(PS[:, (2 * half + k) * 512 + q0:(2 * half + k + 1) * 512], CK[0:SM, kb * P:(kb + 1) * P],
                              CQ[0:SM, j * TILE + q0:(j + 1) * TILE], start=True, stop=True)
                last.then_inc(st_ps[half], 1)

            def values(h, n, half, more):
                j, c = CH[n]
                q = h * NT + (NT - 1 - j)
                if half == 0 and j == c:
                    pe.wait_ge(o_ev, q + 1)
                    if j == 6:
                        pe.wait_ge(mt_ev, h * 2 + 2)
                    if j == 2 and more:
                        pe.wait_ge(mt_ev, h * 2 + 3)
                if half == 0 and n < NT:
                    pe.wait_ge(vh_rdy, h * NT + n + 1)
                if j == c:
                    pe.wait_ge(masked[half], 2 * q + 2)
                else:
                    pe.wait_ge(exp_done[half], h * NCH + n + 1)
                for k in range(2):
                    kb = 2 * half + k
                    for qs in range(kb if j == c else 0, BT):
                        last = mm(PS[:, (6 + j % 2) * 512 + qs * DV:(6 + j % 2) * 512 + (qs + 1) * DV],
                                  PB[half][:, k, qs * P:(qs + 1) * P], VH[:, c * BT + kb, :],
                                  start=(j == c and kb == 0 and qs == 0), stop=(c == 0 and kb == min(BT - 1, qs if j == 0 else BT)),
                                  skip_group_check=True)
                last.then_inc(pv_done[half], 1)

            def maxima(g, n, pair):
                j, c = CH[n]
                if pair == 0 and j == NT - 1:
                    pe.wait_ge(ld_nxt[c], g * SLICE + SLICE)
                for i in range(2):
                    qs = 2 * pair + i
                    w = (qs + 1) * P if j == c else TILE
                    pe.wait_ge(mx_red, g * NMX + n * BT + qs + 1)
                    mm(bank(4 + qs % 2, w), NQ[0:SC, (BT * j + qs) * P:(BT * j + qs + 1) * P],
                       NK[0:SC, c * TILE:c * TILE + w], start=True, stop=True).then_inc(mx_ps, 1)

            def rows(i, grp, evacuated):
                if evacuated is not None:
                    pe.wait_ge(o_ev, evacuated)
                pe.wait_ge(m_rdy, i + 1)
                pe.sem_inc(passed[2], 1)
                nc.tensor.transpose(PS[0:PARTS * NB // 2, 6 * 512:6 * 512 + P // 2].bitcast(bf16),
                                    MP[:, grp, :, :].rearrange("p a b -> p (a b)"), identb[:, :]).then_inc(mt_ps, 1)

            def head(h, more):
                for n in range(NCH):
                    scores(h, n, 1)
                    values(h, n, 0, more)
                    if more:
                        maxima(h + 1, n, 0)
                    if n + 1 < NCH:
                        scores(h, n + 1, 0)
                    elif more:
                        scores(h + 1, 0, 0)
                    values(h, n, 1, more)
                    if more:
                        maxima(h + 1, n, 1)
                        if n == TA_AT:
                            rows(2 * h + 2, 0, h * NT + 4 + FREE_O)
                    if n == TB_AT:
                        rows(2 * h + 1, 1, h * NT + FREE_O)

            for n in range(NCH):
                maxima(0, n, 0)
                maxima(0, n, 1)
                if n == TA_AT:
                    rows(0, 0, None)
            scores(0, 0, 0)
            with pe.Fori(0, H - 1) as h:
                head(h, True)
            head(H - 1, False)

            transposes(2 * NT)
            with pe.Fori(0, NT - 1) as t:
                pe.wait_ge(xt_rdy, t + 2 * NT + 1)
                y_out(t + NT, XT, WO, DK)
                transposes(t + 2 * NT + 1)
            pe.wait_ge(xt_rdy, 3 * NT)
            y_out(2 * NT - 1, XT, WO, DK)
            ffn(NT, 3 * NT, 2 * NT)


def kernel(L0_attn_x, L0_attn_WQ, L0_attn_WK, L0_attn_WV, L0_attn_WO, L0_ffn_W_exp, L0_ffn_b_exp,
           L0_ffn_up_weights, L0_ffn_up_bias, L0_ffn_down_weights, L0_ffn_W_con, L0_ffn_b_con, L0_ffn_down_bias):
    import numpy as np
    import concourse.bacc as bacc
    from concourse.bass_utils import run_bass_kernel_spmd

    def heads_last(w):
        return np.asarray(w).transpose(2, 0, 1).reshape(D, H * DH)

    arrays = {
        "x": np.asarray(L0_attn_x).reshape(S, D),
        "w_exp_t": np.concatenate([np.asarray(L0_ffn_W_exp).T, np.asarray(L0_ffn_b_exp)[:, None]], axis=1),
        "up_w": np.asarray(L0_ffn_up_weights).reshape(STAGES, HID // 2, 4),
        "up_b": np.asarray(L0_ffn_up_bias).reshape(HB, P).T,
        "down_w": np.asarray(L0_ffn_down_weights).reshape(STAGES, HID // 2, 4),
        "w_con": L0_ffn_W_con,
        "b_con": L0_ffn_b_con,
        "down_b": L0_ffn_down_bias,
        "wq": heads_last(L0_attn_WQ),
        "wk": heads_last(L0_attn_WK),
        "wv": heads_last(L0_attn_WV),
        "wo": np.asarray(L0_attn_WO).transpose(0, 2, 1).reshape(H * DH, D),
    }
    arrays = {n: np.ascontiguousarray(a) for n, a in arrays.items()}
    nc = bacc.Bacc("TRN2", target_bir_lowering=False, num_devices=1)
    ins = [nc.dram_tensor(n, a.shape, f32, kind="ExternalInput").ap() for n, a in arrays.items()]
    out = nc.dram_tensor("out", (S, D), f32, kind="ExternalOutput").ap()
    program(nc, *ins, out)
    r = run_bass_kernel_spmd(nc, [arrays], core_ids=[0])
    return r.results[0]["out"].reshape(1, S, D)
```

```python
import concourse.bass as bass
from concourse import mybir
from contextlib import ExitStack

f32 = mybir.dt.float32
bf16 = mybir.dt.bfloat16
ALU = mybir.AluOpType
ACT = mybir.ActivationFunctionType
AX = mybir.AxisListType

S, D, H, DH = 4096, 256, 16, 16
HID, STAGES = 1024, 10
P = 128
TILE = 512
NT = S // TILE
NB = S // P
BT = TILE // P
DK = D // P
HB = HID // P
INNER = 7
DV = DH + 1
PARTS = 3
GROUPS = 6
SC = GROUPS * DH
SM = SC + PARTS
EPS = 1e-5
CH = [(j, c) for j in range(NT - 1, -1, -1) for c in range(j, -1, -1)]
NCH = len(CH)
LAST = {j: max(n for n, (a, _) in enumerate(CH) if a == j) for j in range(NT)}
NMX = NCH * BT
SLICE = 6 * 16
LAG = 2
TB_AT, TA_AT = 4, 30
Q32 = 32


def w_offset(s):
    return 32 * (2 ** s - 1)


W_LEN = w_offset(INNER)
INNER_DMAS = sum(min(HB, P // 2 ** (s + 1)) for s in range(INNER))


def program(nc, x, w_exp_t, up_w, up_b, down_w, w_con, b_con, down_b, wq, wk, wv, wo, out):
    ctx = ExitStack()
    with ctx:
        def sb(name, shape, dt=f32):
            return ctx.enter_context(nc.sbuf_tensor(name, shape, dt))

        def sem(name):
            return ctx.enter_context(nc.semaphore(name))

        X = sb("X", [P, NB, D])
        OA = sb("OA", [P, NB, D])
        V = sb("V", [P, NB, H, DV])
        QK = sb("QK", [P, 4 * S // 2])
        PG = sb("PG", [P, HB, TILE])
        PB = [[PG[:, 4 * i + 2 * k:4 * i + 2 * k + 2, :] for k in range(2)] for i in range(2)]
        SEL = sb("SEL", [P, Q32])
        VH = sb("VH", [P, NB, DV])
        MU = sb("MU", [P, DK, HID])
        MD = sb("MD", [P, HB, D])
        WQ, WK, WV, WO = (sb(n, [P, DK, D]) for n in ("WQ", "WK", "WV", "WO"))
        XN = sb("XN", [P, BT, D])
        XT = sb("XT", [P, DK, TILE])
        G = PG
        SP3 = [sb(f"SP{i}", [P, PARTS, TILE], bf16) for i in range(2)]
        REST = [sb(f"REST{i}", [P, TILE]) for i in range(2)]
        OTS = XT[:, 0, :]
        OS = XN[:, 0, 0:P]
        MASK = sb("MASK", [P, TILE + 3 * P], bf16)
        ident = sb("ident", [P, P])
        identb = sb("identb", [P, P], bf16)
        beta = sb("beta", [P, INNER])
        nbeta = sb("nbeta", [P, INNER])
        DU = sb("DU", [P, 3, 4, 4])
        DD = sb("DD", [P, 3, 4, 4])
        UB = sb("UB", [P, HB])
        GB = sb("GB", [P, HB])
        OB = sb("OB", [P, D])
        OB2 = REST[0][:, 0:D]
        BNS = sb("BNS", [P, NB, 6])
        LN = sb("LN", [P, 4, NB])
        MEAN = sb("MEAN", [P, NB])
        RSTD = sb("RSTD", [P, NB])
        MXP = sb("MXP", [P, NB, NT])
        NEGM = sb("NEGM", [P, 3, NB // 2])
        MP = sb("MP", [P, 2, PARTS, NB // 2], bf16)
        MROW = [sb(f"MROW{i}", [PARTS * NB // 2, P], bf16) for i in range(2)]
        RC = sb("RC", [P, BT])
        PS = ctx.enter_context(nc.psum_tensor("PS", [P, 8 * 512], f32))

        def bank(b, n=512):
            return PS[:, b * 512:b * 512 + n]

        def qk(i):
            return QK[:, i * (S // 2):(i + 1) * (S // 2)].bitcast(bf16)

        CK, CQ, NK, NQ = (qk(i) for i in range(4))
        oa = OA[:, :, :].rearrange("p a b -> p (a b)")
        vv = V[:, :, :, :].rearrange("p a b c -> p (a b c)")
        g_ = G[:, :, :].rearrange("p a b -> p (a b)")

        def fold_scratch(t):
            o = W_LEN
            return dict(w=t[:, 0:o], a=[t[:, o:o + 1024], t[:, o + 1024:o + 2048]],
                        xa=t[:, o + 2048:o + 2560], xb=t[:, o + 2560:o + 3072], t=t[:, o + 3072:o + 4096])

        FU, FD = fold_scratch(oa), fold_scratch(vv)
        BW = D + 1
        WE = g_[:, 0:HB * BW].rearrange("p (b d) -> p b d", b=HB)
        WC = [t[:, :, :].rearrange("p a b -> p (a b)") for t in (XN, XT)]
        T0 = QK[:, 0:HB * BW].rearrange("p (b d) -> p b d", b=HB)
        T1 = QK[:, HB * BW:2 * HB * BW].rearrange("p (b d) -> p b d", b=HB)
        TT = QK[:, 2 * HB * BW:3 * HB * BW].rearrange("p (b d) -> p b d", b=HB)
        AT = g_[:, 2560:2560 + 1024]

        def wc_block(b):
            return WC[b // 4][:, (b % 4) * D:(b % 4 + 1) * D]

        scratch = {n: nc.dram_tensor(f"{n}_parts", [PARTS, H * DH, S], bf16).ap() for n in "qk"}

        const_rdy, beta_rdy, dve_seq, pool_seq = sem("const_rdy"), sem("beta_rdy"), sem("dve_seq"), sem("pool_seq")
        in_up, in_down, in_we, in_wc, in_d, in_proj, in_bias = (
            sem(n) for n in ("in_up", "in_down", "in_we", "in_wc", "in_d", "in_proj", "in_bias"))
        x_in = [sem(f"x_in{t}") for t in range(NT)]
        a_up, a_down = sem("a_up"), sem("a_down")
        fold_ps, fold_ev, mix_a, mix_v, mu_ps, mu_ev = (
            sem(n) for n in ("fold_ps", "fold_ev", "mix_a", "mix_v", "mu_ps", "mu_ev"))
        at_ps, at_ev, md_ps, md_ev, gb_rdy, ob_rdy = (
            sem(n) for n in ("at_ps", "at_ev", "md_ps", "md_ev", "gb_rdy", "ob_rdy"))
        bns_done, ln_step, var_rdy, std_rdy = sem("bns_done"), sem("ln_step"), sem("var_rdy"), sem("std_rdy")
        xn_rdy, tr_ps, xt_rdy, xb_rdy = sem("xn_rdy"), sem("tr_ps"), sem("xt_rdy"), sem("xb_rdy")
        h_ps, gelu_done, y_ps, y_ev = sem("h_ps"), sem("gelu_done"), sem("y_ps"), sem("y_ev")
        qk_ps, hi_done, rest_done, mid_done, parts_done = (
            sem(n) for n in ("qk_ps", "hi_done", "rest_done", "mid_done", "parts_done"))
        parts_out = [sem(f"parts_out{i}") for i in range(2)]
        v_ps, v_ev = sem("v_ps"), sem("v_ev")
        att_init = sem("att_init")
        ld_cur = [sem(f"ld_cur{t}") for t in range(NT)]
        ld_nxt = [sem(f"ld_nxt{t}") for t in range(NT)]
        m_ld = [sem("m_ld0"), sem("m_ld1")]
        st_ps = [sem("st_ps0"), sem("st_ps1")]
        exp_done = [sem("exp_done0"), sem("exp_done1")]
        masked = [sem("masked0"), sem("masked1")]
        pv_done = sem("pv_done")
        vh_rdy, mx_ps, mx_red, m_step, m_rdy, mt_ps, mt_ev = (
            sem(n) for n in ("vh_rdy", "mx_ps", "mx_red", "m_step", "m_rdy", "mt_ps", "mt_ev"))
        ot_ev, os_ps, os_ev, ot_ps = sem("ot_ev"), sem("os_ps"), sem("os_ev"), sem("ot_ps")
        o_rc, o_ev, out_done = sem("o_rc"), sem("o_ev"), sem("out_done")
        passed = [sem(f"passed_{e}") for e in ("pool", "dve", "pe", "sp")]
        FREE_Y, FREE_H, FREE_QK, FREE_REST, FREE_V, FREE_MX, FREE_O, FREE_PB = 2, 4, 4, 2, 2, 2, 1, 2

        x_v = x.rearrange("(t b p) d -> t p b d", p=P, b=BT)
        out_v = out.rearrange("(t b p) d -> t p b d", p=P, b=BT)

        def tile_blocks(t):
            return bass.ds(t * BT, BT) if not isinstance(t, int) else slice(t * BT, (t + 1) * BT)

        def block_at(t, b):
            return bass.ds(t * BT + b, 1) if not isinstance(t, int) else slice(t * BT + b, t * BT + b + 1)

        def inner_product(eng, F, link):
            cur = F["a"][1]
            for s in range(INNER):
                n = 2 ** s
                nxt = F["a"][s % 2]
                o = w_offset(s)
                w = F["w"][:, o:o + HB * n * 4].rearrange("p (b c o e) -> p b o c e", b=HB, c=n, o=2)
                xa, xb = F["xa"][:, 0:HB * n], F["xb"][:, 0:HB * n]
                tmp = F["t"][:, 0:HB * 2 * n].rearrange("p (b o c) -> p b o c", b=HB, o=2)
                new = nxt[:, 0:HB * 2 * n].rearrange("p (b o c) -> p b o c", b=HB, o=2)

                def over_o(t):
                    return t.rearrange("p (b c) -> p b c", b=HB).unsqueeze(2).to_broadcast([P, HB, 2, n])

                eng.tensor_scalar(xa, cur[:, 0:HB * n], nbeta[:, s:s + 1], None, ALU.mult)
                link(eng.tensor_scalar(xb, cur[:, 0:HB * n], beta[:, s:s + 1], None, ALU.mult))
                eng.tensor_tensor(new, w[:, :, :, :, 0], over_o(xa), ALU.mult)
                link(eng.tensor_tensor(tmp, w[:, :, :, :, 1], over_o(xb), ALU.mult))
                link(eng.tensor_tensor(new, new, tmp, ALU.add))
                cur = nxt

        A_FINAL = (INNER - 1) % 2

        def mix_steps(down):
            order = (9, 8, 7) if down else (7, 8, 9)
            wt = DD if down else DU
            for k, s in enumerate(order):
                t = 2 ** (s - INNER)
                for b in range(HB):
                    bit = (b // t) & 1
                    pb = (b // (2 * t)) * t + b % t
                    ia, ib = (bit, 2 + bit) if down else (2 * bit, 2 * bit + 1)
                    yield k, b, b & ~t, b | t, wt[:, s - INNER, pb, ia:ia + 1], wt[:, s - INNER, pb, ib:ib + 1]

        def mix_src(down, k, b):
            if k == 0 and down:
                return wc_block(b)
            w = D if down else BW
            return (T0, T1)[k % 2][:, b, 0:w]

        def mix_dst(down, k, b):
            w = D if down else BW
            return (T1, T0)[k % 2][:, b, 0:w]

        def slot(h, s):
            return (h, s) if s < NCH else (h + 1, s - NCH)

        def tiles_ending(n):
            return [j for j in range(NT) if LAST[j] == n]

        def chain(h, s):
            hh, n = (h, s - 2) if s >= 2 else (h - 1, s - 2 + NCH)
            return [(hh, j) for j in tiles_ending(n)]

        block = ctx.enter_context(nc.Block())

        @block.sync
        def _(sp):
            for i in range(2):
                sp.sem_inc(parts_out[i], 16)

            def inner_weights(src, dst, s, sig):
                n = 2 ** s
                hi = P // (2 * n)
                o = w_offset(s)
                d = dst[:, o:o + HB * n * 4].rearrange("p (b c) -> p b c", b=HB)
                w = src[s].rearrange("(b h c) e -> h b (c e)", b=HB, h=hi)
                if hi <= HB:
                    for k in range(hi):
                        sp.dma_start(d[2 * n * k:2 * n * (k + 1)], w[k:k + 1].to_broadcast([2 * n, HB, n * 4])
                                     ).then_inc(sig, 16)
                else:
                    for b in range(HB):
                        sp.dma_start(d[:, b, :], w[:, b, :].unsqueeze(1).to_broadcast([hi, 2 * n, n * 4])
                                     ).then_inc(sig, 16)

            for s in range(INNER):
                inner_weights(up_w, FU["w"], s, in_up)
            sp.dma_start(WE[:, :, :], w_exp_t.rearrange("(b p) d -> p b d", p=P)).then_inc(in_we, 16)
            for w, d in ((up_w, DU), (down_w, DD)):
                sp.dma_start(d[:, :, :, :], w[INNER:STAGES].rearrange("s (g p) e -> p s g e", p=P)).then_inc(in_d, 16)
            sp.dma_start(UB[:, :], up_b).then_inc(in_d, 16)
            sp.dma_start(OB[:, :], b_con.rearrange("(o d) -> o d", o=1).to_broadcast([P, D])).then_inc(in_bias, 16)
            sp.dma_start(OB2[:, :], down_b.rearrange("(o d) -> o d", o=1).to_broadcast([P, D])).then_inc(in_bias, 16)
            for t in range(NT):
                sp.dma_start(X[:, t * BT:(t + 1) * BT, :], x_v[t]).then_inc(x_in[t], 16)
            for s in range(INNER):
                inner_weights(down_w, FD["w"], s, in_down)
            for i in range(2):
                sp.dma_start(WC[i].rearrange("p (b d) -> p b d", d=D),
                             w_con[i * 512:(i + 1) * 512, :].rearrange("(b p) d -> p b d", p=P)).then_inc(in_wc, 16)
            for d, w in ((WQ, wq), (WK, wk), (WV, wv), (WO, wo)):
                sp.dma_start(d[:, :, :], w.rearrange("(k p) n -> p k n", p=P)).then_inc(in_proj, 16)

            with sp.Fori(0, NT) as t:
                for w in range(4):
                    sp.wait_ge(parts_done, t * 4 + w + 1 + FREE_REST)
                    dst = scratch["q" if w < 2 else "k"][:, (w % 2) * P:(w % 2 + 1) * P, bass.ds(t * TILE, TILE)]
                    sp.dma_start(dst.rearrange("a p t -> p a t"), SP3[w % 2][:, :, :]).then_inc(parts_out[w % 2], 16)
            for i in range(2):
                sp.wait_ge(parts_out[i], 16 * (2 * NT + 1))
            sp.wait_ge(att_init, 2)

            def load_slice(kt, qt, h, j, sig):
                ts = slice(j * TILE, (j + 1) * TILE)
                hs = bass.ds(h * DH, DH) if not isinstance(h, int) else slice(h * DH, (h + 1) * DH)

                def part(name, p0, n, rep):
                    s = scratch[name][p0:p0 + n, hs, ts]
                    return s.to_broadcast([rep, DH, TILE]) if rep > 1 else s

                for dst, name, r0, p0, n, rep in (
                        (kt, "k", 0, 0, 3, 1), (kt, "k", 3, 0, 2, 1), (kt, "k", 5, 0, 1, 1),
                        (qt, "q", 0, 0, 1, 3), (qt, "q", 3, 1, 1, 2), (qt, "q", 5, 2, 1, 1)):
                    g = max(n, rep)
                    sp.dma_start(dst[r0 * DH:(r0 + g) * DH, ts], part(name, p0, n, rep)).then_inc(sig, 16)

            def load_m(i, g):
                sp.wait_ge(mt_ev, i + 1)
                half = NB // 2
                c0 = (1 - g) * (S // 2)
                for p in range(PARTS):
                    sp.dma_start(CQ[SC + p:SC + p + 1, c0:c0 + S // 2], MROW[g][p * half:(p + 1) * half, :]
                                 ).then_inc(m_ld[g], 16)

            for j in range(NT - 1, -1, -1):
                load_slice(NK, NQ, 0, j, ld_nxt[j])
            for j in range(NT - 1, -1, -1):
                load_slice(CK, CQ, 0, j, ld_cur[j])
            for j in range(NT - 1, -1, -1):
                sp.wait_ge(mx_ps, BT * LAST[j] + BT)
                load_slice(NK, NQ, 1, j, ld_nxt[j])
            load_m(0, 0)

            def head_loads(h, more):
                for j in range(NT - 1, -1, -1):
                    sp.wait_ge(st_ps[1], h * NCH + LAST[j] + 1)
                    sp.sem_inc(passed[3], 1)
                    load_slice(CK, CQ, h + 1, j, ld_cur[j])
                    if more:
                        sp.wait_ge(mx_ps, (h + 1) * NMX + BT * LAST[j] + BT)
                        sp.sem_inc(passed[3], 1)
                        load_slice(NK, NQ, h + 2, j, ld_nxt[j])
                    if j == NT - 1:
                        load_m(2 * h + 1, 1)
                    if j == 3:
                        load_m(2 * h + 2, 0)

            with sp.Fori(0, H - 2) as h:
                head_loads(h, True)
            head_loads(H - 2, False)
            load_m(2 * H - 1, 1)

            with sp.Fori(0, NT) as t:
                sp.wait_ge(y_ev, (t + 2 * NT) * BT + BT + FREE_Y)
                sp.dma_start(out.rearrange("(b p) d -> p b d", p=P)[:, bass.ds(t * BT, BT), :],
                             X[:, bass.ds(t * BT, BT), :]).then_inc(out_done, 16)
            sp.wait_ge(out_done, 16 * NT)
            for g in range(2):
                sp.wait_ge(m_ld[g], 48 * H)

        @block.gpsimd
        def _(pool):
            seq = [0]

            def link(ins):
                seq[0] += 1
                ins.then_inc(pool_seq, 1)
                pool.wait_ge(pool_seq, seq[0])

            link(nc.gpsimd.memset(ident[:, :], 0.0))
            nc.gpsimd.affine_select(out=ident[:, :], in_=ident[:, :], compare_op=ALU.not_equal, fill=1.0, base=0,
                                    pattern=[[-1, P]], channel_multiplier=1).then_inc(const_rdy, 1)
            link(nc.gpsimd.memset(MASK[:, :], 0.0))
            nc.gpsimd.affine_select(out=MASK[:, :], in_=MASK[:, :], compare_op=ALU.is_ge, fill=-1e30, base=3 * P,
                                    pattern=[[-1, TILE + 3 * P]], channel_multiplier=1).then_inc(const_rdy, 1)
            pool.wait_ge(const_rdy, 2)
            link(nc.gpsimd.tensor_tensor(SEL[:, :], ident[:, 0:Q32], ident[:, Q32:2 * Q32], ALU.add))
            link(nc.gpsimd.tensor_tensor(SEL[:, :], SEL[:, :], ident[:, 2 * Q32:3 * Q32], ALU.add))
            nc.gpsimd.tensor_tensor(SEL[:, :], SEL[:, :], ident[:, 3 * Q32:4 * Q32], ALU.add).then_inc(const_rdy, 1)
            link(nc.gpsimd.memset(FD["a"][1][:, 0:HB], 1.0))
            pool.wait_ge(beta_rdy, 1)
            pool.wait_ge(in_down, 16 * INNER_DMAS)
            inner_product(nc.gpsimd, FD, link)
            pool.sem_inc(a_down, 1)
            pool.sem_inc(parts_done, FREE_REST)

            def add_bias(t, n):
                pool.wait_ge(xn_rdy, n + 1)
                nc.gpsimd.tensor_tensor(X[:, tile_blocks(t), :], X[:, tile_blocks(t), :],
                                        OB[:, :].unsqueeze(1).to_broadcast([P, BT, D]), ALU.add).then_inc(xb_rdy, 1)

            pool.wait_ge(ob_rdy, 1)
            with pool.Fori(0, NT) as t:
                add_bias(t, t)

            with pool.Fori(0, NT) as t:
                for w in range(4):
                    u = t * 4 + w
                    pool.wait_ge(rest_done, u + 1 + FREE_QK)
                    pool.sem_inc(passed[0], 1)
                    nc.gpsimd.tensor_copy(SP3[w % 2][:, 1, :], REST[w % 2][:, :]).then_inc(mid_done, 1)
                    pool.wait_ge(mid_done, u + 1)
                    nc.gpsimd.tensor_tensor(SP3[w % 2][:, 2, :], REST[w % 2][:, :], SP3[w % 2][:, 1, :],
                                            ALU.subtract).then_inc(parts_done, 1)

            def copy_v(h, j, done):
                pool.wait_ge(pv_done, done + FREE_PB)
                pool.sem_inc(passed[0], 1)
                hs = slice(h, h + 1) if isinstance(h, int) else bass.ds(h, 1)
                nc.gpsimd.tensor_copy(VH[:, j * BT:(j + 1) * BT, :],
                                      V[:, j * BT:(j + 1) * BT, hs, :].rearrange("p b o v -> p b (o v)")
                                      ).then_inc(vh_rdy, 1)

            def head_masks(h, more):
                for j in range(NT - 1, -1, -1):
                    n = CH.index((j, j))
                    for half in range(2):
                        pool.wait_ge(exp_done[half], h * NCH + n + 2)
                        pool.sem_inc(passed[0], 1)
                        for k in range(2):
                            kb = 2 * half + k
                            c0 = kb * P if j else 0
                            tri = PB[n % 2][half][:, k, c0:(kb + 1) * P]
                            nc.gpsimd.affine_select(out=tri, in_=tri, compare_op=ALU.is_ge, fill=0.0, base=c0 - kb * P,
                                                    pattern=[[1, (kb + 1) * P - c0]], channel_multiplier=-1
                                                    ).then_inc(masked[half], 1)
                    if j == NT - 1:
                        copy_v(h, 0, h * NCH)
                    elif more:
                        copy_v(h + 1, j + 1, h * NCH + LAST[j + 1] + 1)

            pool.wait_ge(v_ev, NT * BT + FREE_V)
            for j in range(NT - 1, 0, -1):
                nc.gpsimd.tensor_copy(VH[:, j * BT:(j + 1) * BT, :],
                                      V[:, j * BT:(j + 1) * BT, 0, :]).then_inc(vh_rdy, 1)
            with pool.Fori(0, H - 1) as h:
                head_masks(h, True)
            head_masks(H - 1, False)

            with pool.Fori(0, NT) as t:
                add_bias(t, t + 3 * NT)

        @block.scalar
        def _(act):
            act.sem_inc(gelu_done, FREE_H)
            act.sem_inc(v_ev, FREE_V)
            for b in range(HB):
                act.wait_ge(fold_ps, b + 1)
                nc.scalar.activation(T0[:, b, :], bank(b, BW), ACT.Copy).then_inc(fold_ev, 1)
            act.wait_ge(in_d, 48)
            act.wait_ge(fold_ev, HB)

            def mix_a_side(down):
                for k, b, ia, ib, wa, wb in mix_steps(down):
                    if b == 0 and (k or down):
                        act.wait_ge(mix_v, HB * (k + 3 * down))
                    nc.scalar.activation(TT[:, b, 0:D if down else BW], mix_src(down, k, ia), ACT.Copy,
                                         scale=wa).then_inc(mix_a, 1)

            mix_a_side(0)
            for i in range(4):
                act.wait_ge(mu_ps, i + 1)
                nc.scalar.activation(MU[:, i // 2, (i % 2) * 512:(i % 2 + 1) * 512], bank(i), ACT.Copy
                                     ).then_inc(mu_ev, 1)
            act.wait_ge(in_wc, 32)
            mix_a_side(1)
            for i in range(2):
                act.wait_ge(at_ps, i + 1)
                nc.scalar.activation(AT[:, i * 512:(i + 1) * 512], bank(4 + i), ACT.Copy).then_inc(at_ev, 1)
            for i in range(4):
                act.wait_ge(md_ps, i + 1)
                nc.scalar.activation(MD[:, 2 * i:2 * i + 2, :].rearrange("p a b -> p (a b)"), bank(4 + i), ACT.Copy,
                                     scale=0.5).then_inc(md_ev, 1)

            def std(k):
                act.wait_ge(var_rdy, k + 1)
                nc.scalar.activation(LN[:, 3, :], LN[:, 2, :], ACT.Sqrt).then_inc(std_rdy, 1)

            def gelus(n, y):
                act.wait_ge(y_ps, y * BT + 1)
                for b in range(HB):
                    act.wait_ge(h_ps, n * HB + b + 1)
                    nc.scalar.activation(G[:, b, :], bank(2 + b % 4), ACT.Gelu, bias=GB[:, b:b + 1]
                                         ).then_inc(gelu_done, 1)

            std(0)
            act.wait_ge(gb_rdy, 1)
            act.wait_ge(md_ev, 4)
            with act.Fori(0, NT) as t:
                gelus(t, t)
            std(1)

            with act.Fori(0, NT) as t:
                for w in range(4):
                    act.wait_ge(parts_out[w % 2], (t * 2 + w // 2) * 16 + 16)
                    act.wait_ge(qk_ps, t * 4 + w + 1)
                    nc.scalar.activation(SP3[w % 2][:, 0, :], bank(2 + w), ACT.Copy).then_inc(hi_done, 1)
                for b in range(BT):
                    act.wait_ge(v_ps, t * BT + b + 1)
                    nc.scalar.activation(V[:, bass.ds(t * BT + b, 1), :, 0:DH].rearrange("p o h v -> p (o h) v"),
                                         bank(6 + b % 2, D).rearrange("p (h v) -> p h v", v=DH), ACT.Copy
                                         ).then_inc(v_ev, 1)

            act.sem_inc(exp_done[0], 1)
            act.sem_inc(exp_done[1], 1)

            def exps(h, n):
                j, c = CH[n]
                act.wait_ge(pv_done, h * NCH + n + 1)
                for half in range(2):
                    q0 = 2 * P if (j == c and half and j) else 0
                    act.wait_ge(st_ps[half], h * NCH + n + 1)
                    nc.scalar.activation(
                        PB[n % 2][half][:, :, q0:TILE],
                        PS[:, half * 1024:half * 1024 + 1024].rearrange("p (k q) -> p k q", k=2)[:, :, q0:TILE],
                        ACT.Exp, scale=1.0 / DH ** 0.5).then_inc(exp_done[half], 1)

            def take_sums(h, j):
                act.wait_ge(pv_done, h * NCH + LAST[j] + 1 + FREE_PB)
                act.wait_ge(os_ps, h * NT + (NT - 1 - j) + 1)
                nc.scalar.activation(OTS[:, :], bank(6), ACT.Copy).then_inc(ot_ev, 1)

            exps(0, 0)
            exps(0, 1)

            def turn(h, more):
                for s in range(LAG, NCH + LAG):
                    if s < NCH or more:
                        exps(*slot(h, s))
                    for j in tiles_ending(s - 1):
                        take_sums(h, j)

            with act.Fori(0, H - 1) as h:
                turn(h, True)
            turn(H - 1, False)

            def o_rows(t):
                act.wait_ge(tr_ps, t + 2 * NT)
                nc.scalar.activation(XN[:, :, :], OA[:, tile_blocks(t), :], ACT.Copy).then_inc(xn_rdy, 1)

            act.wait_ge(o_ev, H * NT + FREE_O)
            with act.Fori(0, NT) as t:
                o_rows(t)
            std(2)
            with act.Fori(0, NT) as t:
                gelus(t + NT, t + 2 * NT)

        @block.vector
        def _(dve):
            seq = [0]

            def link(ins):
                seq[0] += 1
                ins.then_inc(dve_seq, 1)
                dve.wait_ge(dve_seq, seq[0])

            dve.sem_inc(y_ev, FREE_Y)
            dve.sem_inc(rest_done, FREE_QK)
            dve.sem_inc(mx_red, FREE_MX)
            dve.sem_inc(o_ev, FREE_O)
            dve.sem_inc(os_ev, 1)
            nc.vector.memset(MXP[:, :, :], -3e38)
            nc.vector.memset(FU["a"][1][:, 0:HB], 1.0)
            dve.wait_ge(const_rdy, 1)
            nc.vector.tensor_copy(identb[:, :], ident[:, :])
            for s in range(INNER):
                v = ident[:, :].rearrange("p (h b l) -> p h b l", b=2, l=2 ** s)[:, :, 1, :]
                last = nc.vector.tensor_reduce(beta[:, s:s + 1], v, AX.XY, ALU.add)
            link(last)
            nc.vector.tensor_scalar(nbeta[:, :], beta[:, :], -1.0, 1.0, ALU.mult, ALU.add).then_inc(beta_rdy, 1)
            dve.wait_ge(beta_rdy, 1)
            dve.wait_ge(in_up, 16 * INNER_DMAS)
            inner_product(nc.vector, FU, link)
            dve.sem_inc(a_up, 1)

            def stats(t, b):
                nc.vector.bn_stats(BNS[:, block_at(t, b), :].rearrange("p o s -> p (o s)"),
                                   X[:, block_at(t, b), :].rearrange("p o d -> p (o d)")).then_inc(bns_done, 1)

            for t in range(NT):
                dve.wait_ge(x_in[t], 16)
                for b in range(BT):
                    stats(t, b)

            def finish_stats(k):
                def step(ins, n):
                    ins.then_inc(ln_step, 1)
                    dve.wait_ge(ln_step, 6 * k + n)
                me, mo = BNS[:, :, 1], BNS[:, :, 4]
                ve, vo = BNS[:, :, 2], BNS[:, :, 5]
                dve.wait_ge(bns_done, NB * (k + 1))
                nc.vector.tensor_tensor(LN[:, 0, :], me, mo, ALU.add)
                step(nc.vector.tensor_tensor(LN[:, 1, :], me, mo, ALU.subtract), 1)
                nc.vector.tensor_scalar(MEAN[:, :], LN[:, 0, :], 0.5, None, ALU.mult)
                step(nc.vector.tensor_tensor(LN[:, 2, :], LN[:, 1, :], LN[:, 1, :], ALU.mult), 2)
                step(nc.vector.tensor_tensor(LN[:, 0, :], ve, vo, ALU.add), 3)
                step(nc.vector.tensor_scalar(LN[:, 1, :], LN[:, 0, :], 1.0 / D, EPS, ALU.mult, ALU.add), 4)
                nc.vector.scalar_tensor_tensor(LN[:, 2, :], LN[:, 2, :], 0.25, LN[:, 1, :], ALU.mult, ALU.add
                                               ).then_inc(var_rdy, 1)
                dve.wait_ge(std_rdy, k + 1)
                step(nc.vector.reciprocal(RSTD[:, :], LN[:, 3, :]), 5)
                step(nc.vector.tensor_copy(LN[:, 0, :], RSTD[:, :]), 6)

            def mix_v_side(down):
                for i, (k, b, ia, ib, wa, wb) in enumerate(mix_steps(down)):
                    if b == 0 and (k or down):
                        dve.wait_ge(mix_v, HB * (k + 3 * down))
                    dve.wait_ge(mix_a, HB * 3 * down + i + 1)
                    nc.vector.scalar_tensor_tensor(mix_dst(down, k, b), mix_src(down, k, ib), wb,
                                                   TT[:, b, 0:D if down else BW], ALU.mult, ALU.add
                                                   ).then_inc(mix_v, 1)

            dve.wait_ge(in_d, 48)
            dve.wait_ge(fold_ev, HB)
            mix_v_side(0)
            dve.wait_ge(mix_v, 3 * HB)
            nc.vector.tensor_tensor(GB[:, :], T1[:, :, D], UB[:, :], ALU.add).then_inc(gb_rdy, 1)
            dve.wait_ge(in_bias, 32)
            link(nc.vector.tensor_tensor(OB[:, :], OB[:, :], OB2[:, :], ALU.add))
            nc.vector.tensor_scalar(OB[:, :], OB[:, :], 0.5, None, ALU.mult).then_inc(ob_rdy, 1)
            dve.wait_ge(mu_ps, 4)
            dve.wait_ge(gb_rdy, 1)
            mix_v_side(1)
            finish_stats(0)

            def normalize(t, n):
                if not (isinstance(n, int) and n == 0):
                    dve.wait_ge(tr_ps, n)
                for b in range(BT):
                    last = nc.vector.tensor_scalar(
                        XN[:, b, :], X[:, block_at(t, b), :].rearrange("p o d -> p (o d)"),
                        MEAN[:, block_at(t, b)], RSTD[:, block_at(t, b)], ALU.subtract, ALU.mult)
                last.then_inc(xn_rdy, 1)

            def take_transposed(n):
                dve.wait_ge(tr_ps, n + 1)
                for k in range(DK):
                    last = nc.vector.tensor_copy(XT[:, k, :], bank(k))
                last.then_inc(xt_rdy, 1)

            def residual(t, y, bias, with_stats):
                if bias is not None:
                    dve.wait_ge(xb_rdy, bias + 1)
                for b in range(BT):
                    dve.wait_ge(y_ps, y * BT + b + 2)
                    xb = X[:, block_at(t, b), :].rearrange("p o d -> p (o d)")
                    nc.vector.tensor_tensor(xb, bank(6 + b % 2, D), xb, ALU.add).then_inc(y_ev, 1)
                if with_stats:
                    for b in range(BT):
                        dve.wait_ge(y_ev, y * BT + b + 1 + FREE_Y)
                        stats(t, b)

            def ffn(n0, y0, bias0, with_stats):
                normalize(0, n0)
                take_transposed(n0)
                with dve.Fori(0, NT - 1) as t:
                    normalize(t + 1, t + n0 + 1)
                    take_transposed(t + n0 + 1)
                    residual(t, t + y0, t + bias0, with_stats)
                residual(NT - 1, NT - 1 + y0, NT - 1 + bias0, with_stats)

            ffn(0, 0, 0, True)
            nc.vector.memset(V[:, :, :, DH:DV], 1.0)
            dve.wait_ge(xn_rdy, NT)
            finish_stats(1)

            def rests(t):
                for w in range(4):
                    u = t * 4 + w
                    dve.wait_ge(hi_done, u + 1)
                    dve.wait_ge(parts_done, u + 1)
                    nc.vector.tensor_tensor(REST[w % 2][:, :], bank(2 + w), SP3[w % 2][:, 0, :], ALU.subtract
                                            ).then_inc(rest_done, 1)

            normalize(0, NT)
            take_transposed(NT)
            with dve.Fori(0, NT - 1) as t:
                rests(t)
                normalize(t + 1, t + NT + 1)
                take_transposed(t + NT + 1)
            rests(NT - 1)
            nc.vector.memset(CK[96:SM, :], 1.0).then_inc(att_init, 1)
            dve.wait_ge(v_ev, NT * BT + FREE_V)
            nc.vector.memset(bank(6), 0.0).then_inc(att_init, 1)

            def maximum(g, n, qs):
                j, c = CH[n]
                dve.wait_ge(mx_ps, g * NMX + n * BT + qs + 1)
                dst = MXP[:, BT * j + qs, c:c + 1]
                if j == c:
                    w = (qs + 1) * P
                    s = bank(4 + qs % 2, w)
                    dve.sem_inc(passed[1], 1)
                    nc.vector.tensor_tensor_reduce(out=s, in0=s, in1=MASK[:, 3 * P - qs * P:3 * P - qs * P + w],
                                                   scale=1.0, scalar=-3e38, op0=ALU.add, op1=ALU.max,
                                                   accum_out=dst).then_inc(mx_red, 1)
                else:
                    nc.vector.tensor_reduce(dst, bank(4 + qs % 2), AX.X, ALU.max).then_inc(mx_red, 1)

            def split_maxima(g, grp):
                i = 2 * g + grp
                nb = NB // 2
                r = [NEGM[:, k, :] for k in range(3)]
                mp = [MP[:, grp, k, :] for k in range(PARTS)]

                def step(ins, k):
                    ins.then_inc(m_step, 1)
                    dve.wait_ge(m_step, i * 5 + k)
                dve.wait_ge(mx_red, g * NMX + (LAST[4] + 1) * BT * (1 - grp) + NMX * grp + FREE_MX)
                step(nc.vector.tensor_reduce(r[0], MXP[:, (1 - grp) * nb:(2 - grp) * nb, :], AX.X, ALU.max,
                                             negate=True), 1)
                step(nc.vector.tensor_copy(mp[0], r[0]), 2)
                step(nc.vector.tensor_tensor(r[1], r[0], mp[0], ALU.subtract), 3)
                step(nc.vector.tensor_copy(mp[1], r[1]), 4)
                step(nc.vector.tensor_tensor(r[2], r[1], mp[1], ALU.subtract), 5)
                nc.vector.tensor_copy(mp[2], r[2]).then_inc(m_rdy, 1)

            def take_rows(i, grp):
                dve.wait_ge(mt_ps, i + 1)
                nc.vector.tensor_copy(MROW[grp][:, :], PS[0:PARTS * NB // 2, 7 * 512 + 256:7 * 512 + 256 + P // 2].bitcast(bf16)
                                      ).then_inc(mt_ev, 1)

            def take_added(h, j):
                q = h * NT + (NT - 1 - j)
                dve.wait_ge(os_ps, q + 2)
                nc.vector.tensor_copy(OS[:, :], bank(7, P)).then_inc(os_ev, 1)

            def take_o(h, j):
                q = h * NT + (NT - 1 - j)
                O = PS[:, 7 * 512 + P:7 * 512 + 2 * P].rearrange("p (b v) -> p b v", v=Q32)
                dve.wait_ge(ot_ps, q + 1)
                dve.wait_ge(o_ev, q + FREE_O)
                nc.vector.reciprocal(RC[:, :], O[:, :, DH]).then_inc(o_rc, 1)
                dve.wait_ge(o_rc, q + 1)
                hs = slice(h * DH, (h + 1) * DH) if isinstance(h, int) else bass.ds(h * DH, DH)
                nc.vector.tensor_tensor(OA[:, j * BT:(j + 1) * BT, hs], O[:, :, 0:DH],
                                        RC[:, :].unsqueeze(2).to_broadcast([P, BT, DH]), ALU.mult).then_inc(o_ev, 1)

            for n in range(NCH):
                for qs in range(BT):
                    maximum(0, n, qs)
                if n == LAST[4]:
                    split_maxima(0, 0)
                if n == TA_AT - LAG:
                    take_rows(0, 0)
            split_maxima(0, 1)

            def turn(h, more):
                for s in range(LAG, NCH + LAG):
                    done = chain(h, s)
                    if more:
                        maximum(h + 1, s - LAG, 0)
                    for d in done:
                        take_added(*d)
                    if more:
                        maximum(h + 1, s - LAG, 1)
                    for d in done:
                        take_o(*d)
                    if more:
                        maximum(h + 1, s - LAG, 2)
                        maximum(h + 1, s - LAG, 3)
                        if s - LAG == LAST[4]:
                            split_maxima(h + 1, 0)
                        if s == TA_AT:
                            take_rows(2 * h + 2, 0)
                    if s == TB_AT:
                        take_rows(2 * h + 1, 1)
                if more:
                    split_maxima(h + 1, 1)

            with dve.Fori(0, H - 1) as h:
                turn(h, True)
            turn(H - 1, False)

            take_transposed(2 * NT)
            with dve.Fori(0, NT - 1) as t:
                residual(t, t + NT, None, True)
                take_transposed(t + 2 * NT + 1)
            residual(NT - 1, 2 * NT - 1, None, True)
            finish_stats(2)
            ffn(3 * NT, 2 * NT, NT, False)

        @block.tensor
        def _(pe):
            mm = nc.tensor.matmul
            pe.sem_inc(y_ps, 1)
            pe.sem_inc(pv_done, FREE_PB)
            pe.sem_inc(os_ps, 1)
            pe.wait_ge(a_up, 1)
            pe.wait_ge(in_we, 16)
            AU, AD = FU["a"][A_FINAL], FD["a"][A_FINAL]
            for b in range(HB):
                mm(bank(b, BW), AU[:, b * P:(b + 1) * P], WE[:, b, :], start=True, stop=True).then_inc(fold_ps, 1)
            pe.wait_ge(fold_ev, HB)
            pe.wait_ge(mix_v, 3 * HB)
            for i in range(4):
                for k in range(4):
                    last = nc.tensor.transpose(PS[:, i * 512 + k * P:i * 512 + (k + 1) * P],
                                               T1[:, (i % 2) * 4 + k, (i // 2) * P:(i // 2 + 1) * P], ident[:, :])
                last.then_inc(mu_ps, 1)
            pe.wait_ge(a_down, 1)
            for i in range(2):
                for k in range(4):
                    b = 4 * i + k
                    last = nc.tensor.transpose(PS[:, (4 + i) * 512 + k * P:(4 + i) * 512 + (k + 1) * P],
                                               AD[:, b * P:(b + 1) * P], ident[:, :])
                last.then_inc(at_ps, 1)
            pe.wait_ge(at_ev, 2)
            pe.wait_ge(mix_v, 6 * HB)
            for i in range(4):
                for k in range(2):
                    b = 2 * i + k
                    last = mm(PS[:, (4 + i) * 512 + k * D:(4 + i) * 512 + (k + 1) * D], AT[:, b * P:(b + 1) * P],
                              T1[:, b, 0:D], start=True, stop=True)
                last.then_inc(md_ps, 1)

            def transposes(n):
                pe.wait_ge(xn_rdy, n + 1)
                if not (isinstance(n, int) and n == 0):
                    pe.wait_ge(xt_rdy, n)
                for k in range(DK):
                    for b in range(BT):
                        last = nc.tensor.transpose(PS[:, k * 512 + b * P:k * 512 + (b + 1) * P],
                                                   XN[:, b, k * P:(k + 1) * P], ident[:, :])
                last.then_inc(tr_ps, 1)

            def up(n, x):
                pe.wait_ge(xt_rdy, x + 1)
                for b in range(HB):
                    pe.wait_ge(gelu_done, n * HB + b + 1)
                    for k in range(DK):
                        last = mm(bank(2 + b % 4), MU[:, k, b * P:(b + 1) * P], XT[:, k, :],
                                  start=(k == 0), stop=(k == DK - 1))
                    last.then_inc(h_ps, 1)

            def y_out(y, lhs, rhs, nk):
                for b in range(BT):
                    pe.wait_ge(y_ev, y * BT + b + 1)
                    for k in range(nk):
                        last = mm(bank(6 + b % 2, D), lhs[:, k, b * P:(b + 1) * P], rhs[:, k, :],
                                  start=(k == 0), stop=(k == nk - 1))
                    last.then_inc(y_ps, 1)

            def down(n, y):
                pe.wait_ge(gelu_done, n * HB + HB + FREE_H)
                y_out(y, G, MD, HB)

            def ffn(n0, x0, y0):
                transposes(x0)
                with pe.Fori(0, NT - 1) as t:
                    up(t + n0, t + x0)
                    transposes(t + x0 + 1)
                    down(t + n0, t + y0)
                up(NT - 1 + n0, NT - 1 + x0)
                down(NT - 1 + n0, NT - 1 + y0)

            pe.wait_ge(mu_ev, 4)
            pe.wait_ge(md_ev, 4)
            ffn(0, 0, 0)

            pe.wait_ge(in_proj, 64)

            def project(t):
                pe.wait_ge(xt_rdy, t + NT + 1)
                for w in range(4):
                    pe.wait_ge(rest_done, t * 4 + w + 1)
                    for k in range(DK):
                        last = mm(bank(2 + w), (WQ if w < 2 else WK)[:, k, (w % 2) * P:(w % 2 + 1) * P], XT[:, k, :],
                                  start=(k == 0), stop=(k == DK - 1))
                    last.then_inc(qk_ps, 1)
                for b in range(BT):
                    pe.wait_ge(v_ev, t * BT + b + 1)
                    for k in range(DK):
                        last = mm(bank(6 + b % 2, D), XT[:, k, b * P:(b + 1) * P], WV[:, k, :],
                                  start=(k == 0), stop=(k == DK - 1))
                    last.then_inc(v_ps, 1)

            transposes(NT)
            with pe.Fori(0, NT - 1) as t:
                project(t)
                transposes(t + NT + 1)
            project(NT - 1)
            pe.wait_ge(rest_done, 4 * NT + FREE_QK)
            pe.wait_ge(v_ev, NT * BT + FREE_V)
            pe.wait_ge(att_init, 2)
            pe.wait_ge(const_rdy, 3)

            def scores(h, n, half):
                j, c = CH[n]
                if half == 0 and j == NT - 1:
                    pe.wait_ge(ld_cur[c], h * SLICE + SLICE)
                if half == 0 and n == 0:
                    pe.wait_ge(m_ld[0], h * 48 + 48)
                if half == 0 and n == LAST[4] + 1:
                    pe.wait_ge(m_ld[1], h * 48 + 48)
                q0 = 2 * P if (j == c and half and j) else 0
                pe.wait_ge(exp_done[half], h * NCH + n + 1)
                for k in range(2):
                    kb = c * BT + 2 * half + k
                    last = mm(PS[:, (2 * half + k) * 512 + q0:(2 * half + k + 1) * 512], CK[0:SM, kb * P:(kb + 1) * P],
                              CQ[0:SM, j * TILE + q0:(j + 1) * TILE], start=True, stop=True)
                last.then_inc(st_ps[half], 1)

            def values(h, n, part):
                j, c = CH[n]
                if part == 1:
                    pass
                elif j == c:
                    q = h * NT + (NT - 1 - j)
                    if not (isinstance(h, int) and h == 0 and n == 0):
                        pe.wait_ge(ot_ev, q)
                    for half in range(2):
                        pe.wait_ge(masked[half], 2 * q + 2)
                else:
                    pe.wait_ge(exp_done[1], h * NCH + n + 2)
                if n < NT and part == 0:
                    pe.wait_ge(vh_rdy, h * NT + n + 1)
                for kb in range(BT):
                    first = kb * P if (j == c and j) else 0
                    q0, q1 = max(first, part * TILE // 2), (part + 1) * TILE // 2
                    if q0 < q1:
                        last = mm(PS[kb * Q32:kb * Q32 + DV, 6 * 512 + q0:6 * 512 + q1], VH[:, c * BT + kb, :],
                                  PB[n % 2][kb // 2][:, kb % 2, q0:q1], start=(j == c and q0 == first),
                                  stop=(c == 0), skip_group_check=True)
                if part:
                    last.then_inc(pv_done, 1)

            def add_tiles(h, j, more):
                q = h * NT + (NT - 1 - j)
                if j == NT - 1:
                    pe.wait_ge(mt_ev, 2 * h + 2)
                if j == 3 and more:
                    pe.wait_ge(mt_ev, 2 * h + 3)
                pe.wait_ge(ot_ev, q + 1)
                pe.wait_ge(o_ev, q + FREE_O)
                for b in range(BT):
                    last = mm(PS[b * Q32:(b + 1) * Q32, 7 * 512:7 * 512 + P], SEL[:, :], OTS[:, b * P:(b + 1) * P],
                              start=True, stop=True, skip_group_check=True)
                last.then_inc(os_ps, 1)

            def turn_sums(h, j):
                q = h * NT + (NT - 1 - j)
                pe.wait_ge(os_ev, q + 2)
                nc.tensor.transpose(PS[:, 7 * 512 + P:7 * 512 + 2 * P], OS[:, :], ident[:, :]).then_inc(ot_ps, 1)

            def maximum(g, n, qs):
                j, c = CH[n]
                if qs == 0 and j == NT - 1:
                    pe.wait_ge(ld_nxt[c], g * SLICE + SLICE)
                w = (qs + 1) * P if j == c else TILE
                pe.wait_ge(mx_red, g * NMX + n * BT + qs + 1)
                mm(bank(4 + qs % 2, w), NQ[0:SC, (BT * j + qs) * P:(BT * j + qs + 1) * P],
                   NK[0:SC, c * TILE:c * TILE + w], start=True, stop=True).then_inc(mx_ps, 1)

            def rows(i, grp, evacuated):
                if evacuated is not None:
                    pe.wait_ge(o_ev, evacuated)
                pe.wait_ge(m_rdy, i + 1)
                pe.sem_inc(passed[2], 1)
                nc.tensor.transpose(PS[0:PARTS * NB // 2, 7 * 512 + 256:7 * 512 + 256 + P // 2].bitcast(bf16),
                                    MP[:, grp, :, :].rearrange("p a b -> p (a b)"), identb[:, :]).then_inc(mt_ps, 1)

            def turn(h, more):
                for s in range(LAG, NCH + LAG):
                    hs, n = slot(h, s)
                    ahead = s < NCH or more
                    done = chain(h, s)
                    if more:
                        maximum(h + 1, s - LAG, 0)
                    if ahead:
                        scores(hs, n, 0)
                    for d in done:
                        add_tiles(*d, more)
                    if more:
                        maximum(h + 1, s - LAG, 1)
                    if ahead:
                        scores(hs, n, 1)
                    for d in done:
                        turn_sums(*d)
                    if more:
                        maximum(h + 1, s - LAG, 2)
                    if s <= NCH or more:
                        values(*slot(h, s - 1), 0)
                    if more:
                        maximum(h + 1, s - LAG, 3)
                    if s <= NCH or more:
                        values(*slot(h, s - 1), 1)
                    if more and s == TA_AT:
                        rows(2 * h + 2, 0, h * NT + 4 + FREE_O)
                    if s == TB_AT:
                        rows(2 * h + 1, 1, h * NT + FREE_O)

            for n in range(NCH):
                for qs in range(BT):
                    maximum(0, n, qs)
                if n == TA_AT - LAG:
                    rows(0, 0, None)
            scores(0, 0, 0)
            scores(0, 0, 1)
            scores(0, 1, 0)
            scores(0, 1, 1)
            values(0, 0, 0)
            values(0, 0, 1)
            with pe.Fori(0, H - 1) as h:
                turn(h, True)
            turn(H - 1, False)

            transposes(2 * NT)
            with pe.Fori(0, NT - 1) as t:
                pe.wait_ge(xt_rdy, t + 2 * NT + 1)
                y_out(t + NT, XT, WO, DK)
                transposes(t + 2 * NT + 1)
            pe.wait_ge(xt_rdy, 3 * NT)
            y_out(2 * NT - 1, XT, WO, DK)
            ffn(NT, 3 * NT, 2 * NT)


def kernel(L0_attn_x, L0_attn_WQ, L0_attn_WK, L0_attn_WV, L0_attn_WO, L0_ffn_W_exp, L0_ffn_b_exp,
           L0_ffn_up_weights, L0_ffn_up_bias, L0_ffn_down_weights, L0_ffn_W_con, L0_ffn_b_con, L0_ffn_down_bias):
    import numpy as np
    import concourse.bacc as bacc
    from concourse.bass_utils import run_bass_kernel_spmd

    def heads_last(w):
        return np.asarray(w).transpose(2, 0, 1).reshape(D, H * DH)

    arrays = {
        "x": np.asarray(L0_attn_x).reshape(S, D),
        "w_exp_t": np.concatenate([np.asarray(L0_ffn_W_exp).T, np.asarray(L0_ffn_b_exp)[:, None]], axis=1),
        "up_w": np.asarray(L0_ffn_up_weights).reshape(STAGES, HID // 2, 4),
        "up_b": np.asarray(L0_ffn_up_bias).reshape(HB, P).T,
        "down_w": np.asarray(L0_ffn_down_weights).reshape(STAGES, HID // 2, 4),
        "w_con": L0_ffn_W_con,
        "b_con": L0_ffn_b_con,
        "down_b": L0_ffn_down_bias,
        "wq": heads_last(L0_attn_WQ),
        "wk": heads_last(L0_attn_WK),
        "wv": heads_last(L0_attn_WV),
        "wo": np.asarray(L0_attn_WO).transpose(0, 2, 1).reshape(H * DH, D),
    }
    arrays = {n: np.ascontiguousarray(a) for n, a in arrays.items()}
    nc = bacc.Bacc("TRN2", target_bir_lowering=False, num_devices=1)
    ins = [nc.dram_tensor(n, a.shape, f32, kind="ExternalInput").ap() for n, a in arrays.items()]
    out = nc.dram_tensor("out", (S, D), f32, kind="ExternalOutput").ap()
    program(nc, *ins, out)
    r = run_bass_kernel_spmd(nc, [arrays], core_ids=[0])
    return r.results[0]["out"].reshape(1, S, D)
```

```python
import concourse.bass as bass
from concourse import mybir
from contextlib import ExitStack

f32 = mybir.dt.float32
bf16 = mybir.dt.bfloat16
ALU = mybir.AluOpType
ACT = mybir.ActivationFunctionType
AX = mybir.AxisListType

S, D, H, DH = 4096, 256, 16, 16
HID, STAGES = 1024, 10
P = 128
TILE = 512
NT = S // TILE
NB = S // P
BT = TILE // P
DK = D // P
HB = HID // P
INNER = 7
DV = DH + 1
PARTS = 3
GROUPS = 6
SC = GROUPS * DH
SM = SC + PARTS
EPS = 1e-5
CH = [(j, c) for j in range(NT - 1, -1, -1) for c in range(j, -1, -1)]
NCH = len(CH)
LAST = {j: max(n for n, (a, _) in enumerate(CH) if a == j) for j in range(NT)}
NMX = NCH * BT
MX0 = [[(CH.index((j, c)), qs) for c in range(j, -1, -1) for qs in range(BT)] for j in range(NT)]
MX0_ALL = [i for m in MX0 for i in m]
MX0_START = [sum(len(m) for m in MX0[:j]) for j in range(NT)]
MX0_FIRST = (BT - 1) * BT
MX0_LATE = 2
MX0_ALONE = MX0_START[NT - 2] + MX0_FIRST + MX0_LATE
H_AHEAD = 6
SLICE = 6 * 16
LAG = 2
SB_AT, SA_AT = 2, 28
TB_AT, TA_AT = 4, 29
Q32 = 32


def w_offset(s):
    return 32 * (2 ** s - 1)


UP_BY_POOL, DOWN_BY_POOL = 3, 3
W_LEN = w_offset(INNER)
INNER_DMAS = [min(2 ** (s + 1), P // 2 ** (s + 1)) for s in range(INNER)]


def program(nc, x, w_exp_t, up_w, up_b, down_w, w_con, b_con, down_b, wq, wk, wv, wo, out):
    ctx = ExitStack()
    with ctx:
        def sb(name, shape, dt=f32):
            return ctx.enter_context(nc.sbuf_tensor(name, shape, dt))

        def sem(name):
            return ctx.enter_context(nc.semaphore(name))

        X = sb("X", [P, NB, D])
        OA = sb("OA", [P, NB, D])
        V = sb("V", [P, NB, H, DV])
        QK = sb("QK", [P, 4 * S // 2])
        PG = sb("PG", [P, HB, TILE])
        PB = [[PG[:, 4 * i + 2 * k:4 * i + 2 * k + 2, :] for k in range(2)] for i in range(2)]
        SEL = sb("SEL", [P, Q32])
        VH = sb("VH", [P, NB, DV])
        MU = sb("MU", [P, DK, HID])
        MD = sb("MD", [P, HB, D])
        WQ, WK, WV, WO = (sb(n, [P, DK, D]) for n in ("WQ", "WK", "WV", "WO"))
        XN = sb("XN", [P, BT, D])
        XT = sb("XT", [P, DK, TILE])
        G = PG
        SP3 = [OA[:, 16 + 3 * i:19 + 3 * i, :].rearrange("p a b -> p (a b)").bitcast(bf16)
               .rearrange("p (k t) -> p k t", k=PARTS) for i in range(4)]
        REST = [sb(f"REST{i}", [P, TILE]) for i in range(2)]
        XN2A, XT2A = (OA[:, 4 * i:4 * i + 4, :] for i in range(2))
        OTS = XT[:, 0, :]
        OS = XN[:, 0, 0:P]
        MASK = sb("MASK", [P, TILE + 3 * P], bf16)
        ident = sb("ident", [P, P])
        identb = sb("identb", [P, P], bf16)
        beta = sb("beta", [P, INNER])
        nbeta = sb("nbeta", [P, INNER])
        DU = sb("DU", [P, 3, 4, 4])
        DD = sb("DD", [P, 3, 4, 4])
        UB = sb("UB", [P, HB])
        GB = sb("GB", [P, HB])
        OB = sb("OB", [P, D])
        OB2 = REST[0][:, 0:D]
        BNS = sb("BNS", [P, NB, 6])
        LN = sb("LN", [P, 4, NB])
        MEAN = sb("MEAN", [P, NB])
        RSTD = sb("RSTD", [P, NB])
        MXP = sb("MXP", [P, NB, NT])
        NEGM = sb("NEGM", [P, 3, NB // 2])
        MP = sb("MP", [P, 2, PARTS, NB // 2], bf16)
        MROW = [sb(f"MROW{i}", [PARTS * NB // 2, P], bf16) for i in range(2)]
        RC = sb("RC", [P, BT])
        PS = ctx.enter_context(nc.psum_tensor("PS", [P, 8 * 512], f32))

        def bank(b, n=512):
            return PS[:, b * 512:b * 512 + n]

        def y_bank(b):
            return bank(6 + b % 2, D)

        TURNS = []
        for t in range(NT + 1):
            h = [("h", t * HB + b) for b in range(HB)] if t < NT else []
            TURNS += h[:H_AHEAD] + ([("qk", (t - 1) * 4 + w) for w in range(4)] if t else []) + h[H_AHEAD:]

        def turn_bank(kind, i):
            return 2 + TURNS.index((kind, i)) % 2

        def before_in_bank(kind, i):
            n = TURNS.index((kind, i))
            return TURNS[n - 2] if n >= 2 else None

        def qk(i):
            return QK[:, i * (S // 2):(i + 1) * (S // 2)].bitcast(bf16)

        XN2B = QK[:, 0:BT * D].rearrange("p (b d) -> p b d", b=BT)
        XT2B = QK[:, BT * D:2 * BT * D].rearrange("p (k t) -> p k t", k=DK)
        XT2A = XT2A.rearrange("p a b -> p (a b)").rearrange("p (k t) -> p k t", k=DK)
        CK, CQ, NK, NQ = (qk(i) for i in range(4))
        oa = OA[:, :, :].rearrange("p a b -> p (a b)")
        vv = V[:, :, :, :].rearrange("p a b c -> p (a b c)")
        g_ = G[:, :, :].rearrange("p a b -> p (a b)")

        def fold_scratch(t):
            o = W_LEN
            return dict(w=t[:, 0:o], a=[t[:, o:o + 1024], t[:, o + 1024:o + 2048]],
                        xa=t[:, o + 2048:o + 2560], xb=t[:, o + 2560:o + 3072], t=t[:, o + 3072:o + 4096])

        FU, FD = fold_scratch(oa), fold_scratch(vv)
        BW = D + 1
        WE = g_[:, 0:HB * BW].rearrange("p (b d) -> p b d", b=HB)
        WC = MD
        T0 = QK[:, 0:HB * BW].rearrange("p (b d) -> p b d", b=HB)
        T1 = QK[:, HB * BW:2 * HB * BW].rearrange("p (b d) -> p b d", b=HB)
        TT = QK[:, 2 * HB * BW:3 * HB * BW].rearrange("p (b d) -> p b d", b=HB)
        AT = oa[:, 2 * BT * D:2 * BT * D + 1024]

        def wc_block(b):
            return WC[:, b, :]

        scratch = {n: nc.dram_tensor(f"{n}_parts", [PARTS, H * DH, S], bf16).ap() for n in "qk"}

        const_rdy, beta_rdy, dve_seq, pool_seq = sem("const_rdy"), sem("beta_rdy"), sem("dve_seq"), sem("pool_seq")
        in_up, in_down = ([sem(f"{n}{s}") for s in range(INNER)] for n in ("in_up", "in_down"))
        in_we, in_wc, in_d, in_proj, in_bias = (
            sem(n) for n in ("in_we", "in_wc", "in_d", "in_proj", "in_bias"))
        x_in = [sem(f"x_in{t}") for t in range(NT)]
        a_up, a_down = sem("a_up"), sem("a_down")
        fold_ps, fold_ev, mix_a, mix_v, mu_ps, mu_ev = (
            sem(n) for n in ("fold_ps", "fold_ev", "mix_a", "mix_v", "mu_ps", "mu_ev"))
        at_ps, at_ev, md_ps, md_ev, gb_rdy, ob_rdy = (
            sem(n) for n in ("at_ps", "at_ev", "md_ps", "md_ev", "gb_rdy", "ob_rdy"))
        bns_done, ln_step, var_rdy, std_rdy = sem("bns_done"), sem("ln_step"), sem("var_rdy"), sem("std_rdy")
        xn_rdy, tr_ps, xt_rdy, xb_rdy = sem("xn_rdy"), sem("tr_ps"), sem("xt_rdy"), sem("xb_rdy")
        or_rdy = sem("or_rdy")
        h_ps, gelu_done, y_ps, y_ev = sem("h_ps"), sem("gelu_done"), sem("y_ps"), sem("y_ev")
        qk_ps, hi_done, rest_done, mid_done, parts_done = (
            sem(n) for n in ("qk_ps", "hi_done", "rest_done", "mid_done", "parts_done"))
        parts_out = [sem(f"parts_out{i}") for i in range(4)]
        v_ps, v_ev = sem("v_ps"), sem("v_ev")
        att_init = sem("att_init")
        ld_cur = [sem(f"ld_cur{t}") for t in range(NT)]
        ld_nxt = [sem(f"ld_nxt{t}") for t in range(NT)]
        m_ld = [sem("m_ld0"), sem("m_ld1")]
        st_ps = [sem("st_ps0"), sem("st_ps1")]
        exp_done = [sem("exp_done0"), sem("exp_done1")]
        masked = [sem("masked0"), sem("masked1")]
        pv_done = sem("pv_done")
        vh_rdy, mx_ps, mx_red, m_step, m_rdy, mt_ps, mt_ev = (
            sem(n) for n in ("vh_rdy", "mx_ps", "mx_red", "m_step", "m_rdy", "mt_ps", "mt_ev"))
        ot_ev, os_ps, os_ev, ot_ps = sem("ot_ev"), sem("os_ps"), sem("os_ev"), sem("ot_ps")
        o_rc, o_ev, out_done = sem("o_rc"), sem("o_ev"), sem("out_done")
        passed = [sem(f"passed_{e}") for e in ("pool", "dve", "pe", "sp")]
        FREE_Y, FREE_H, FREE_QK, FREE_REST, FREE_V, FREE_MX, FREE_O, FREE_PB = 2, 4, 4, 2, 2, 2, 1, 2

        def seq_f(t):
            return 2 * t - 1 if t else 0

        def seq_p(t):
            return 2 * t + 2 if t < NT - 1 else 2 * NT - 1

        def seq_w(t):
            return 2 * NT + 2 * t

        def seq_f2(t):
            return 2 * NT + 2 * t + 1

        def y_w(t):
            return NT + 2 * t - 1

        def y_f2(t):
            return NT + 2 * t + 2

        Y_W0, Y_LAST = NT, 3 * NT - 1

        def mx0_beside(t):
            late = [(t - 2, i) for i in range(MX0_FIRST, len(MX0[t - 2]))] if t >= 2 else []
            if t == NT:
                late = late[0:MX0_LATE]
            soon = [(t - 1, i) for i in range(min(MX0_FIRST, len(MX0[t - 1])))] if 1 <= t < NT else []
            return late, soon

        x_v = x.rearrange("(t b p) d -> t p b d", p=P, b=BT)
        out_v = out.rearrange("(t b p) d -> t p b d", p=P, b=BT)

        def tile_blocks(t):
            return bass.ds(t * BT, BT) if not isinstance(t, int) else slice(t * BT, (t + 1) * BT)

        def block_at(t, b):
            return bass.ds(t * BT + b, 1) if not isinstance(t, int) else slice(t * BT + b, t * BT + b + 1)

        def inner_product(eng, F, link, loaded):
            cur = F["a"][1]
            for s in range(INNER):
                n = 2 ** s
                nxt = F["a"][s % 2]
                o = w_offset(s)
                w = F["w"][:, o:o + HB * n * 4].rearrange("p (b c o e) -> p b o c e", b=HB, c=n, o=2)
                xa, xb = F["xa"][:, 0:HB * n], F["xb"][:, 0:HB * n]
                tmp = F["t"][:, 0:HB * 2 * n].rearrange("p (b o c) -> p b o c", b=HB, o=2)
                new = nxt[:, 0:HB * 2 * n].rearrange("p (b o c) -> p b o c", b=HB, o=2)

                def over_o(t):
                    return t.rearrange("p (b c) -> p b c", b=HB).unsqueeze(2).to_broadcast([P, HB, 2, n])

                eng.wait_ge(loaded[s], 16 * INNER_DMAS[s])
                eng.tensor_scalar(xa, cur[:, 0:HB * n], nbeta[:, s:s + 1], None, ALU.mult)
                link(eng.tensor_scalar(xb, cur[:, 0:HB * n], beta[:, s:s + 1], None, ALU.mult))
                eng.tensor_tensor(new, w[:, :, :, :, 0], over_o(xa), ALU.mult)
                link(eng.tensor_tensor(tmp, w[:, :, :, :, 1], over_o(xb), ALU.mult))
                link(eng.tensor_tensor(new, new, tmp, ALU.add))
                cur = nxt

        A_FINAL = (INNER - 1) % 2

        def mix_steps(down):
            order = (9, 8, 7) if down else (7, 8, 9)
            wt = DD if down else DU
            for k, s in enumerate(order):
                t = 2 ** (s - INNER)
                for b in range(HB):
                    bit = (b // t) & 1
                    pb = (b // (2 * t)) * t + b % t
                    ia, ib = (bit, 2 + bit) if down else (2 * bit, 2 * bit + 1)
                    yield k, b, b & ~t, b | t, wt[:, s - INNER, pb, ia:ia + 1], wt[:, s - INNER, pb, ib:ib + 1]

        def mix_src(down, k, b):
            if k == 0 and down:
                return wc_block(b)
            w = D if down else BW
            return (T0, T1)[k % 2][:, b, 0:w]

        def mix_dst(down, k, b):
            w = D if down else BW
            return (T1, T0)[k % 2][:, b, 0:w]

        def o_bank(j, c0=0, n=512):
            return PS[:, (6 + j % 2) * 512 + c0:(6 + j % 2) * 512 + c0 + n]

        TURNED = PS[0:PARTS * NB // 2, 6 * 512 + 256:6 * 512 + 256 + P // 2].bitcast(bf16)

        def slot(h, s):
            return (h, s) if s < NCH else (h + 1, s - NCH)

        def tiles_ending(n):
            return [j for j in range(NT) if LAST[j] == n]

        def chain(h, s):
            hh, n = (h, s - 2) if s >= 2 else (h - 1, s - 2 + NCH)
            return [(hh, j) for j in tiles_ending(n)]

        def inner_weights(eng, src, dst, s, sig):
            n = 2 ** s
            hi = P // (2 * n)
            o = w_offset(s)
            d = dst[:, o:o + HB * n * 4].rearrange("p (b c) -> p b c", b=HB)
            w = src[s].rearrange("(b h c) e -> h b (c e)", b=HB, h=hi)
            if hi < 2 * n:
                for k in range(hi):
                    eng.dma_start(d[2 * n * k:2 * n * (k + 1)], w[k:k + 1].to_broadcast([2 * n, HB, n * 4])
                                  ).then_inc(sig, 16)
            else:
                for r in range(2 * n):
                    eng.dma_start(d[r:P:2 * n], w).then_inc(sig, 16)

        block = ctx.enter_context(nc.Block())

        @block.sync
        def _(sp):
            for w in range(4):
                sp.sem_inc(parts_out[w], 16)

            for s in range(INNER):
                if s != UP_BY_POOL:
                    inner_weights(sp, up_w, FU["w"], s, in_up[s])
            sp.dma_start(WE[:, :, :], w_exp_t.rearrange("(b p) d -> p b d", p=P)).then_inc(in_we, 16)
            for w, d in ((up_w, DU), (down_w, DD)):
                sp.dma_start(d[:, :, :, :], w[INNER:STAGES].rearrange("s (g p) e -> p s g e", p=P)).then_inc(in_d, 16)
            sp.dma_start(UB[:, :], up_b).then_inc(in_d, 16)
            for t in range(NT):
                sp.dma_start(X[:, t * BT:(t + 1) * BT, :], x_v[t]).then_inc(x_in[t], 16)
                if t == 1:
                    sp.dma_start(WC[:, :, :], w_con.rearrange("(b p) d -> p b d", p=P)).then_inc(in_wc, 16)
                    for s in range(DOWN_BY_POOL, INNER):
                        inner_weights(sp, down_w, FD["w"], s, in_down[s])
                    sp.wait_ge(in_down[INNER - 1], 16 * INNER_DMAS[INNER - 1])
            for b, d in ((b_con, OB[:, :]), (down_b, OB2)):
                sp.dma_start(d, b.rearrange("(o d) -> o d", o=1).to_broadcast([P, D])).then_inc(in_bias, 16)
            for d, w in ((WQ, wq), (WK, wk), (WV, wv), (WO, wo)):
                sp.dma_start(d[:, :, :], w.rearrange("(k p) n -> p k n", p=P)).then_inc(in_proj, 16)

            def load_slice(kt, qt, h, j, sig):
                ts = slice(j * TILE, (j + 1) * TILE)
                hs = bass.ds(h * DH, DH) if not isinstance(h, int) else slice(h * DH, (h + 1) * DH)

                def part(name, p0, n, rep):
                    s = scratch[name][p0:p0 + n, hs, ts]
                    return s.to_broadcast([rep, DH, TILE]) if rep > 1 else s

                for dst, name, r0, p0, n, rep in (
                        (kt, "k", 0, 0, 3, 1), (kt, "k", 3, 0, 2, 1), (kt, "k", 5, 0, 1, 1),
                        (qt, "q", 0, 0, 1, 3), (qt, "q", 3, 1, 1, 2), (qt, "q", 5, 2, 1, 1)):
                    g = max(n, rep)
                    if dst is not None:
                        sp.dma_start(dst[r0 * DH:(r0 + g) * DH, ts], part(name, p0, n, rep)).then_inc(sig, 16)

            for t in range(NT):
                for w in range(4):
                    sp.wait_ge(parts_done, t * 4 + w + 1 + FREE_REST)
                    dst = scratch["q" if w < 2 else "k"][:, (w % 2) * P:(w % 2 + 1) * P, t * TILE:(t + 1) * TILE]
                    sp.dma_start(dst.rearrange("a p t -> p a t"), SP3[w][:, :, :]).then_inc(parts_out[w], 16)
                for w in range(4):
                    sp.wait_ge(parts_out[w], 16 * (t + 2))
                load_slice(NK, NQ, 0, t, ld_nxt[t])
                load_slice(CK, CQ, 0, t, ld_cur[t])
                if t:
                    sp.wait_ge(mx_ps, MX0_START[t])
                    load_slice(None, NQ, 1, t - 1, ld_nxt[t - 1])

            def load_m(i, g):
                sp.wait_ge(mt_ev, i + 1)
                half = NB // 2
                c0 = (1 - g) * (S // 2)
                sp.dma_start(CQ[SC:SM, c0:c0 + S // 2].rearrange("p (b t) -> p b t", b=half), MROW[g][:, :]
                             ).then_inc(m_ld[g], 16)

            for c in range(NT - 1, -1, -1):
                sp.wait_ge(mx_ps, MX0_START[NT - 1] + BT * (NT - c))
                if c == 0:
                    load_m(0, 0)
                load_slice(NK, None, 1, c, ld_nxt[c])
            load_slice(None, NQ, 1, NT - 1, ld_nxt[NT - 1])

            def head_loads(h, more):
                for j in range(NT - 1, -1, -1):
                    sp.wait_ge(st_ps[1], h * NCH + LAST[j] + 1)
                    sp.sem_inc(passed[3], 1)
                    load_slice(CK, CQ, h + 1, j, ld_cur[j])
                    if more:
                        sp.wait_ge(mx_ps, (h + 1) * NMX + BT * LAST[j] + BT)
                        sp.sem_inc(passed[3], 1)
                        load_slice(NK, NQ, h + 2, j, ld_nxt[j])
                    if j == NT - 1:
                        load_m(2 * h + 1, 1)
                    if j == 3:
                        load_m(2 * h + 2, 0)

            with sp.Fori(0, H - 2) as h:
                head_loads(h, True)
            head_loads(H - 2, False)
            load_m(2 * H - 1, 1)

            with sp.Fori(0, NT - 1) as t:
                sp.wait_ge(y_ev, y_f2(t) * BT + BT + FREE_Y)
                sp.dma_start(out.rearrange("(b p) d -> p b d", p=P)[:, bass.ds(t * BT, BT), :],
                             X[:, bass.ds(t * BT, BT), :]).then_inc(out_done, 16)
            sp.wait_ge(y_ev, 3 * NT * BT + FREE_Y)
            sp.dma_start(out.rearrange("(b p) d -> p b d", p=P)[:, NB - BT:NB, :], X[:, NB - BT:NB, :]
                         ).then_inc(out_done, 16)
            sp.wait_ge(out_done, 16 * NT)
            for g in range(2):
                sp.wait_ge(m_ld[g], 16 * H)

        @block.gpsimd
        def _(pool):
            seq = [0]

            def link(ins):
                seq[0] += 1
                ins.then_inc(pool_seq, 1)
                pool.wait_ge(pool_seq, seq[0])

            inner_weights(nc.gpsimd, up_w, FU["w"], UP_BY_POOL, in_up[UP_BY_POOL])
            link(nc.gpsimd.memset(ident[:, :], 0.0))
            nc.gpsimd.affine_select(out=ident[:, :], in_=ident[:, :], compare_op=ALU.not_equal, fill=1.0, base=0,
                                    pattern=[[-1, P]], channel_multiplier=1).then_inc(const_rdy, 1)
            link(nc.gpsimd.memset(MASK[:, :], 0.0))
            nc.gpsimd.affine_select(out=MASK[:, :], in_=MASK[:, :], compare_op=ALU.is_ge, fill=-1e30, base=3 * P,
                                    pattern=[[-1, TILE + 3 * P]], channel_multiplier=1).then_inc(const_rdy, 1)
            pool.wait_ge(const_rdy, 2)
            link(nc.gpsimd.tensor_tensor(SEL[:, :], ident[:, 0:Q32], ident[:, Q32:2 * Q32], ALU.add))
            link(nc.gpsimd.tensor_tensor(SEL[:, :], SEL[:, :], ident[:, 2 * Q32:3 * Q32], ALU.add))
            nc.gpsimd.tensor_tensor(SEL[:, :], SEL[:, :], ident[:, 3 * Q32:4 * Q32], ALU.add).then_inc(const_rdy, 1)
            link(nc.gpsimd.memset(FD["a"][1][:, 0:HB], 1.0))
            for s in range(DOWN_BY_POOL):
                inner_weights(nc.gpsimd, down_w, FD["w"], s, in_down[s])
            pool.wait_ge(beta_rdy, 1)
            inner_product(nc.gpsimd, FD, link, in_down)
            pool.sem_inc(a_down, 1)

            def add_bias(t, n):
                pool.wait_ge(xn_rdy, n + 1)
                nc.gpsimd.tensor_tensor(X[:, tile_blocks(t), :], X[:, tile_blocks(t), :],
                                        OB[:, :].unsqueeze(1).to_broadcast([P, BT, D]), ALU.add).then_inc(xb_rdy, 1)

            pool.wait_ge(md_ps, 4)
            nc.gpsimd.memset(CK[96:SM, :], 1.0).then_inc(att_init, 1)
            pool.wait_ge(att_init, 1)
            pool.wait_ge(ob_rdy, 1)
            for t in range(NT):
                add_bias(t, seq_f(t))

            def copy_v(h, j, done):
                pool.wait_ge(pv_done, done + FREE_PB)
                pool.sem_inc(passed[0], 1)
                hs = slice(h, h + 1) if isinstance(h, int) else bass.ds(h, 1)
                nc.gpsimd.tensor_copy(VH[:, j * BT:(j + 1) * BT, :],
                                      V[:, j * BT:(j + 1) * BT, hs, :].rearrange("p b o v -> p b (o v)")
                                      ).then_inc(vh_rdy, 1)

            def head_masks(h, more):
                for j in range(NT - 1, -1, -1):
                    n = CH.index((j, j))
                    for half in range(2):
                        pool.wait_ge(exp_done[half], h * NCH + n + 2)
                        pool.sem_inc(passed[0], 1)
                        for k in range(2):
                            kb = 2 * half + k
                            c0 = kb * P if j else 0
                            tri = PB[n % 2][half][:, k, c0:(kb + 1) * P]
                            nc.gpsimd.affine_select(out=tri, in_=tri, compare_op=ALU.is_ge, fill=0.0, base=c0 - kb * P,
                                                    pattern=[[1, (kb + 1) * P - c0]], channel_multiplier=-1
                                                    ).then_inc(masked[half], 1)
                    if j == NT - 1:
                        copy_v(h, 0, h * NCH)
                    elif more:
                        copy_v(h + 1, j + 1, h * NCH + LAST[j + 1] + 1)

            pool.wait_ge(v_ev, NT * BT + FREE_V)
            for j in range(NT - 1, 0, -1):
                nc.gpsimd.tensor_copy(VH[:, j * BT:(j + 1) * BT, :],
                                      V[:, j * BT:(j + 1) * BT, 0, :]).then_inc(vh_rdy, 1)
            with pool.Fori(0, H - 1) as h:
                head_masks(h, True)
            head_masks(H - 1, False)

            with pool.Fori(0, NT) as t:
                add_bias(t, t + 2 * NT)

        @block.scalar
        def _(act):
            act.sem_inc(gelu_done, FREE_H)
            act.sem_inc(v_ev, FREE_V)
            for b in range(HB):
                act.wait_ge(fold_ps, b + 1)
                nc.scalar.activation(T0[:, b, :], bank(b, BW), ACT.Copy).then_inc(fold_ev, 1)
            act.wait_ge(in_d, 48)
            act.wait_ge(fold_ev, HB)

            def std(k, cols):
                act.wait_ge(var_rdy, k + 1)
                nc.scalar.activation(LN[:, 3, cols], LN[:, 2, cols], ACT.Sqrt).then_inc(std_rdy, 1)

            def mix_a_side(down, stages):
                for k, b, ia, ib, wa, wb in mix_steps(down):
                    if k not in stages:
                        continue
                    if b == 0 and (k or down):
                        act.wait_ge(mix_v, HB * (k + 3 * down))
                    nc.scalar.activation(TT[:, b, 0:D if down else BW], mix_src(down, k, ia), ACT.Copy,
                                         scale=wa).then_inc(mix_a, 1)

            std(0, slice(0, 2 * BT))
            mix_a_side(0, range(3))
            for i in range(4):
                act.wait_ge(mu_ps, i + 1)
                nc.scalar.activation(MU[:, i // 2, (i % 2) * 512:(i % 2 + 1) * 512], bank(2 + i), ACT.Copy
                                     ).then_inc(mu_ev, 1)
            def gelus(n, y, blocks=range(HB)):
                act.wait_ge(y_ps, y * BT + 1)
                for b in blocks:
                    act.wait_ge(h_ps, n * HB + b + 1)
                    src = bank(turn_bank("h", n * HB + b) if isinstance(n, int) and n < NT else 2 + b % 4)
                    nc.scalar.activation(G[:, b, :], src, ACT.Gelu, bias=GB[:, b:b + 1]
                                         ).then_inc(gelu_done, 1)


            act.wait_ge(gb_rdy, 1)

            def take_md():
                for i in range(2):
                    act.wait_ge(at_ps, i + 1)
                    nc.scalar.activation(AT[:, i * 512:(i + 1) * 512], bank(6 + i), ACT.Copy).then_inc(at_ev, 1)
                for i in range(4):
                    act.wait_ge(md_ps, i + 1)
                    nc.scalar.activation(MD[:, 2 * i:2 * i + 2, :].rearrange("p a b -> p (a b)"), bank(5 + i % 3), ACT.Copy,
                                         scale=0.5).then_inc(md_ev, 1)

            def high_parts(t):
                for w in range(4):
                    act.wait_ge(parts_out[w], t * 16 + 16)
                    act.wait_ge(qk_ps, t * 4 + w + 1)
                    nc.scalar.activation(SP3[w][:, 0, :], bank(turn_bank("qk", t * 4 + w)), ACT.Copy).then_inc(hi_done, 1)

            def take_v(t):
                for b in range(BT):
                    act.wait_ge(v_ps, t * BT + b + 1)
                    nc.scalar.activation(V[:, t * BT + b, :, 0:DH],
                                         y_bank(b).rearrange("p (h v) -> p h v", v=DH), ACT.Copy
                                         ).then_inc(v_ev, 1)

            for t in range(NT + 1):
                if t == NT:
                    std(t + 1, slice(0, BT))
                if t == 0:
                    act.wait_ge(in_wc, 16)
                    for k in range(3):
                        gelus(0, 0, (2 * k, 2 * k + 1))
                        mix_a_side(1, (k,))
                elif t < NT:
                    gelus(t, t, (0, 1))
                    std(t + 1, slice(0, BT))
                    gelus(t, t, range(2, H_AHEAD))
                if t:
                    high_parts(t - 1)
                if t < NT:
                    gelus(t, t, range(H_AHEAD, HB))
                if t == 0:
                    take_md()
                    std(1, slice(0, NB - 2 * BT))
                if t:
                    take_v(t - 1)

            act.sem_inc(exp_done[0], 1)
            act.sem_inc(exp_done[1], 1)

            def exps(h, n):
                j, c = CH[n]
                act.wait_ge(pv_done, h * NCH + n + 1)
                for half in range(2):
                    q0 = 2 * P if (j == c and half and j) else 0
                    act.wait_ge(st_ps[half], h * NCH + n + 1)
                    nc.scalar.activation(
                        PB[n % 2][half][:, :, q0:TILE],
                        PS[:, half * 1024:half * 1024 + 1024].rearrange("p (k q) -> p k q", k=2)[:, :, q0:TILE],
                        ACT.Exp, scale=1.0 / DH ** 0.5).then_inc(exp_done[half], 1)

            def take_sums(h, j):
                act.wait_ge(pv_done, h * NCH + LAST[j] + 1 + FREE_PB)
                act.wait_ge(os_ps, h * NT + (NT - 1 - j) + 1)
                nc.scalar.activation(OTS[:, :], o_bank(j), ACT.Copy).then_inc(ot_ev, 1)

            exps(0, 0)
            exps(0, 1)

            def turn(h, more):
                for s in range(LAG, NCH + LAG):
                    if s < NCH or more:
                        exps(*slot(h, s))
                    for j in tiles_ending(s - 1):
                        take_sums(h, j)

            with act.Fori(0, H - 1) as h:
                turn(h, True)
            turn(H - 1, False)

            def o_rows(t):
                if not isinstance(t, int):
                    act.wait_ge(tr_ps, seq_w(t - 1) + 1)
                nc.scalar.activation(XN2B[:, :, :], OA[:, tile_blocks(t), :], ACT.Copy).then_inc(or_rdy, 1)

            act.wait_ge(o_ev, H * NT + FREE_O)
            o_rows(0)
            std(NT + 2, slice(0, BT))
            with act.Fori(0, NT - 1) as t:
                o_rows(t + 1)
                gelus(t + NT, y_f2(t) - 1)
                std(t + NT + 3, slice(0, BT))
            gelus(2 * NT - 1, Y_LAST)

        @block.vector
        def _(dve):
            seq = [0]

            def link(ins):
                seq[0] += 1
                ins.then_inc(dve_seq, 1)
                dve.wait_ge(dve_seq, seq[0])

            dve.sem_inc(y_ev, FREE_Y)
            dve.sem_inc(rest_done, FREE_QK)
            dve.sem_inc(parts_done, FREE_REST)
            dve.sem_inc(mx_red, FREE_MX)
            dve.sem_inc(o_ev, FREE_O)
            dve.sem_inc(os_ev, 1)
            nc.vector.memset(MXP[:, :, :], -3e38)
            nc.vector.memset(FU["a"][1][:, 0:HB], 1.0)
            dve.wait_ge(const_rdy, 1)
            nc.vector.tensor_copy(identb[:, :], ident[:, :])
            for s in range(INNER):
                v = ident[:, :].rearrange("p (h b l) -> p h b l", b=2, l=2 ** s)[:, :, 1, :]
                last = nc.vector.tensor_reduce(beta[:, s:s + 1], v, AX.XY, ALU.add)
            link(last)
            nc.vector.tensor_scalar(nbeta[:, :], beta[:, :], -1.0, 1.0, ALU.mult, ALU.add).then_inc(beta_rdy, 1)
            dve.wait_ge(beta_rdy, 1)
            inner_product(nc.vector, FU, link, in_up)
            dve.sem_inc(a_up, 1)

            def stats(t, b):
                nc.vector.bn_stats(BNS[:, block_at(t, b), :].rearrange("p o s -> p (o s)"),
                                   X[:, block_at(t, b), :].rearrange("p o d -> p (o d)")).then_inc(bns_done, 1)

            def first_stats(t):
                dve.wait_ge(x_in[t], 16)
                for b in range(BT):
                    stats(t, b)

            for t in range(2):
                first_stats(t)

            def finish_stats(k, cols, w, done, before_std=()):
                def step(ins, n):
                    ins.then_inc(ln_step, 1)
                    dve.wait_ge(ln_step, 5 * k + n)
                L = [LN[:, i, 0:w] for i in range(4)]
                me, mo = BNS[:, cols, 1], BNS[:, cols, 4]
                ve, vo = BNS[:, cols, 2], BNS[:, cols, 5]
                dve.wait_ge(bns_done, done)
                nc.vector.tensor_tensor(L[0], me, mo, ALU.add)
                step(nc.vector.tensor_tensor(L[1], me, mo, ALU.subtract), 1)
                nc.vector.tensor_scalar(MEAN[:, cols], L[0], 0.5, None, ALU.mult)
                step(nc.vector.tensor_tensor(L[2], L[1], L[1], ALU.mult), 2)
                step(nc.vector.tensor_tensor(L[0], ve, vo, ALU.add), 3)
                step(nc.vector.tensor_scalar(L[1], L[0], 1.0 / D, EPS, ALU.mult, ALU.add), 4)
                nc.vector.scalar_tensor_tensor(L[2], L[2], 0.25, L[1], ALU.mult, ALU.add).then_inc(var_rdy, 1)
                for item in before_std:
                    maximum0(*item)
                dve.wait_ge(std_rdy, k + 1)
                step(nc.vector.reciprocal(RSTD[:, cols], L[3]), 5)

            def normalize(dst, t, before):
                if before is not None:
                    dve.wait_ge(tr_ps, before)
                for b in range(BT):
                    last = nc.vector.tensor_scalar(
                        dst[:, b, :], X[:, block_at(t, b), :].rearrange("p o d -> p (o d)"),
                        MEAN[:, block_at(t, b)], RSTD[:, block_at(t, b)], ALU.subtract, ALU.mult)
                last.then_inc(xn_rdy, 1)

            def mix_v_side(down):
                for i, (k, b, ia, ib, wa, wb) in enumerate(mix_steps(down)):
                    if b == 0 and (k or down):
                        dve.wait_ge(mix_v, HB * (k + 3 * down))
                    dve.wait_ge(mix_a, HB * 3 * down + i + 1)
                    nc.vector.scalar_tensor_tensor(mix_dst(down, k, b), mix_src(down, k, ib), wb,
                                                   TT[:, b, 0:D if down else BW], ALU.mult, ALU.add
                                                   ).then_inc(mix_v, 1)

            finish_stats(0, slice(0, 2 * BT), 2 * BT, 2 * BT)
            normalize(XN, 0, None)
            dve.wait_ge(in_d, 48)
            dve.wait_ge(fold_ev, HB)
            mix_v_side(0)
            dve.wait_ge(mix_v, 3 * HB)
            nc.vector.tensor_tensor(GB[:, :], T1[:, :, D], UB[:, :], ALU.add).then_inc(gb_rdy, 1)

            def take_transposed(dst, seq):
                dve.wait_ge(tr_ps, seq + 1)
                for k in range(DK):
                    last = nc.vector.tensor_copy(dst[:, k, :], bank(k))
                last.then_inc(xt_rdy, 1)

            def residual_block(t, y, b, beside=()):
                for item in beside:
                    maximum0(*item)
                dve.wait_ge(y_ps, y * BT + b + 2)
                xb = X[:, block_at(t, b), :].rearrange("p o d -> p (o d)")
                nc.vector.tensor_tensor(xb, y_bank(b), xb, ALU.add).then_inc(y_ev, 1)

            def residual_stats(t, y):
                for b in range(BT):
                    dve.wait_ge(y_ev, y * BT + b + 1 + FREE_Y)
                    stats(t, b)

            def rests(t):
                def rest(w):
                    u = t * 4 + w
                    dve.wait_ge(hi_done, u + 1)
                    dve.wait_ge(parts_done, u + 1)
                    nc.vector.tensor_tensor(REST[w % 2][:, :], bank(turn_bank("qk", u)), SP3[w][:, 0, :],
                                            ALU.subtract).then_inc(rest_done, 1)

                rest(0)
                for w in range(4):
                    u = t * 4 + w
                    dve.wait_ge(rest_done, u + 1 + FREE_QK)
                    nc.vector.tensor_copy(SP3[w][:, 1, :], REST[w % 2][:, :]).then_inc(mid_done, 1)
                    if w < 3:
                        rest(w + 1)
                    dve.wait_ge(mid_done, u + 1)
                    nc.vector.tensor_tensor(SP3[w][:, 2, :], REST[w % 2][:, :], SP3[w][:, 1, :],
                                            ALU.subtract).then_inc(parts_done, 1)

            def maximum0(j, i):
                n, qs = MX0[j][i]
                maximum(MX0_START[j] + i, n, qs)

            def maximum(seq, n, qs):
                j, c = CH[n]
                dve.wait_ge(mx_ps, seq + 1)
                dst = MXP[:, BT * j + qs, c:c + 1]
                if j == c:
                    w = (qs + 1) * P
                    s = bank(4 + qs % 2, w)
                    dve.sem_inc(passed[1], 1)
                    nc.vector.tensor_tensor_reduce(out=s, in0=s, in1=MASK[:, 3 * P - qs * P:3 * P - qs * P + w],
                                                   scale=1.0, scalar=-3e38, op0=ALU.add, op1=ALU.max,
                                                   accum_out=dst).then_inc(mx_red, 1)
                else:
                    nc.vector.tensor_reduce(dst, bank(4 + qs % 2), AX.X, ALU.max).then_inc(mx_red, 1)

            take_transposed(XT, seq_f(0))
            dve.wait_ge(in_bias, 32)
            link(nc.vector.tensor_tensor(OB[:, :], OB[:, :], OB2[:, :], ALU.add))
            nc.vector.tensor_scalar(OB[:, :], OB[:, :], 0.5, None, ALU.mult).then_inc(ob_rdy, 1)
            for t in range(NT + 1):
                late, soon = mx0_beside(t)
                if t == 0:
                    dve.wait_ge(mu_ps, 4)
                    dve.wait_ge(gb_rdy, 1)
                    dve.wait_ge(in_wc, 16)
                    mix_v_side(1)
                else:
                    finish_stats(t + 1, slice((t - 1) * BT, t * BT), BT, NB + t * BT, late[0:4])
                    normalize(XN2A, t - 1, seq_p(t - 2) + 1 if t > 1 else None)
                for item in late[4:8]:
                    maximum0(*item)
                if t:
                    take_transposed(XT2A, seq_p(t - 1))
                for item in late[8:]:
                    maximum0(*item)
                if t:
                    rests(t - 1)
                if t + 1 < NT:
                    normalize(XN, t + 1, seq_f(t) + 1)
                if t == 0:
                    for i in range(2, NT):
                        first_stats(i)
                if t + 1 < NT:
                    take_transposed(XT, seq_f(t + 1))
                if t == 0:
                    finish_stats(1, slice(2 * BT, NB), NB - 2 * BT, NB)
                    dve.wait_ge(at_ps, 2)
                    nc.vector.memset(V[:, :, :, DH:DV], 1.0)
                if t < NT:
                    dve.wait_ge(xb_rdy, t + 1)
                    for b in range(BT):
                        residual_block(t, t, b, soon[BT * (b - 1):BT * b] if b else ())
                    residual_stats(t, t)
            for seq in range(MX0_ALONE, NMX):
                n, qs = MX0_ALL[seq]
                maximum(seq, n, qs)
            dve.wait_ge(v_ev, NT * BT + FREE_V)
            nc.vector.memset(PS[:, 6 * 512:8 * 512], 0.0).then_inc(att_init, 1)

            def split_step(g, grp, k):
                i = 2 * g + grp
                nb = NB // 2
                r = [NEGM[:, a, :] for a in range(3)]
                mp = [MP[:, grp, a, :] for a in range(PARTS)]
                if k == 0:
                    ready = (LAST[4] + 1) * BT if grp == 0 and not isinstance(g, int) else NMX
                    dve.wait_ge(mx_red, g * NMX + ready + FREE_MX)
                    ins = nc.vector.tensor_reduce(r[0], MXP[:, (1 - grp) * nb:(2 - grp) * nb, :], AX.X, ALU.max,
                                                  negate=True)
                else:
                    dve.wait_ge(m_step, i * 5 + k)
                    a = k // 2
                    if k % 2:
                        ins = nc.vector.tensor_copy(mp[a], r[a])
                    else:
                        ins = nc.vector.tensor_tensor(r[a], r[a - 1], mp[a - 1], ALU.subtract)
                ins.then_inc(m_step if k < 5 else m_rdy, 1)

            def take_rows(i, grp):
                dve.wait_ge(mt_ps, i + 1)
                nc.vector.tensor_copy(MROW[grp][:, :], TURNED).then_inc(mt_ev, 1)

            def take_added(h, j):
                q = h * NT + (NT - 1 - j)
                dve.wait_ge(os_ps, q + 2)
                nc.vector.tensor_copy(OS[:, :], o_bank(j, 0, P)).then_inc(os_ev, 1)

            def take_o(h, j):
                q = h * NT + (NT - 1 - j)
                O = o_bank(j, P, P).rearrange("p (b v) -> p b v", v=Q32)
                dve.wait_ge(ot_ps, q + 1)
                dve.wait_ge(o_ev, q + FREE_O)
                nc.vector.reciprocal(RC[:, :], O[:, :, DH]).then_inc(o_rc, 1)
                dve.wait_ge(o_rc, q + 1)
                hs = slice(h * DH, (h + 1) * DH) if isinstance(h, int) else bass.ds(h * DH, DH)
                nc.vector.tensor_tensor(OA[:, j * BT:(j + 1) * BT, hs], O[:, :, 0:DH],
                                        RC[:, :].unsqueeze(2).to_broadcast([P, BT, DH]), ALU.mult).then_inc(o_ev, 1)

            for k in range(6):
                split_step(0, 0, k)
            take_rows(0, 0)

            def head_maximum(g, n, qs):
                maximum(g * NMX + n * BT + qs, n, qs)

            def turn(h, more):
                for s in range(LAG, NCH + LAG):
                    done = chain(h, s)
                    for qs in range(BT):
                        if more:
                            head_maximum(h + 1, s - LAG, qs)
                        if qs == 1:
                            for d in done:
                                take_added(*d)
                        if qs == 3:
                            for d in done:
                                take_o(*d)
                        if 0 <= BT * (s - SB_AT) + qs < 6:
                            split_step(h, 1, BT * (s - SB_AT) + qs)
                        if more and 0 <= BT * (s - SA_AT) + qs < 6:
                            split_step(h + 1, 0, BT * (s - SA_AT) + qs)
                    if more and s == TA_AT:
                        take_rows(2 * h + 2, 0)
                    if s == TB_AT:
                        take_rows(2 * h + 1, 1)

            with dve.Fori(0, H - 1) as h:
                turn(h, True)
            turn(H - 1, False)

            def projected(t, y):
                for b in range(BT):
                    residual_block(t, y, b)
                residual_stats(t, y)
                finish_stats(t + NT + 2, tile_blocks(t), BT, 2 * NB + t * BT + BT)

            take_transposed(XT2B, seq_w(0))
            projected(0, Y_W0)
            normalize(XN, 0, None)
            take_transposed(XT, seq_f2(0))
            with dve.Fori(0, NT - 1) as t:
                take_transposed(XT2B, seq_w(t + 1))
                projected(t + 1, y_w(t + 1))
                normalize(XN, t + 1, seq_f2(t) + 1)
                dve.wait_ge(xb_rdy, t + NT + 1)
                for b in range(BT - 1):
                    residual_block(t, y_f2(t), b)
                take_transposed(XT, seq_f2(t + 1))
                residual_block(t, y_f2(t), BT - 1)
            dve.wait_ge(xb_rdy, 2 * NT)
            for b in range(BT):
                residual_block(NT - 1, Y_LAST, b)

        @block.tensor
        def _(pe):
            mm = nc.tensor.matmul
            pe.sem_inc(y_ps, 1)
            pe.sem_inc(pv_done, FREE_PB)
            pe.sem_inc(os_ps, 1)
            pe.wait_ge(a_up, 1)
            pe.wait_ge(in_we, 16)
            AU, AD = FU["a"][A_FINAL], FD["a"][A_FINAL]
            for b in range(HB):
                mm(bank(b, BW), AU[:, b * P:(b + 1) * P], WE[:, b, :], start=True, stop=True).then_inc(fold_ps, 1)
            pe.wait_ge(fold_ev, HB)
            def transposes(src, src_rdy, n, seq):
                pe.wait_ge(src_rdy, n + 1)
                if not (isinstance(seq, int) and seq == 0):
                    pe.wait_ge(xt_rdy, seq)
                for k in range(DK):
                    for b in range(BT):
                        last = nc.tensor.transpose(PS[:, k * 512 + b * P:k * 512 + (b + 1) * P],
                                                   src[:, b, k * P:(k + 1) * P], ident[:, :])
                last.then_inc(tr_ps, 1)

            def turn_free(kind, i):
                before = before_in_bank(kind, i)
                if before and before[0] == "h":
                    pe.wait_ge(gelu_done, before[1] + 1 + FREE_H)
                elif before:
                    pe.wait_ge(rest_done, before[1] + 1 + FREE_QK)

            def fold_down():
                pe.wait_ge(a_down, 1)
                for i in range(2):
                    for k in range(4):
                        b = 4 * i + k
                        last = nc.tensor.transpose(PS[:, (6 + i) * 512 + k * P:(6 + i) * 512 + (k + 1) * P],
                                                   AD[:, b * P:(b + 1) * P], ident[:, :])
                    last.then_inc(at_ps, 1)
                pe.wait_ge(at_ev, 2)
                pe.wait_ge(mix_v, 6 * HB)
                for i in range(4):
                    if i == 3:
                        pe.wait_ge(md_ev, 1)
                    for k in range(2):
                        b = 2 * i + k
                        last = mm(bank(5 + i % 3)[:, k * D:(k + 1) * D], AT[:, b * P:(b + 1) * P],
                                  T1[:, b, 0:D], start=True, stop=True)
                    last.then_inc(md_ps, 1)

            def up_block(b, dst, beside=()):
                for k in range(DK):
                    last = mm(dst, MU[:, k, b * P:(b + 1) * P], XT[:, k, :],
                              start=(k == 0), stop=(k == DK - 1))
                    if k < DK - 1:
                        for item in beside:
                            maximum0(*item)
                last.then_inc(h_ps, 1)

            def y_block(b, lhs, rhs, nk, beside=()):
                for k in range(nk):
                    last = mm(y_bank(b), lhs[:, k, b * P:(b + 1) * P], rhs[:, k, :],
                              start=(k == 0), stop=(k == nk - 1))
                    if k % 2:
                        for item in beside[k // 2:k // 2 + 1]:
                            maximum0(*item)
                last.then_inc(y_ps, 1)

            def maximum0(j, i):
                seq = MX0_START[j] + i
                if i == 0:
                    pe.wait_ge(ld_nxt[j], SLICE)
                pe.wait_ge(mx_red, seq + 1)
                maximum(seq, *MX0[j][i])

            def maximum(seq, n, qs):
                j, c = CH[n]
                w = (qs + 1) * P if j == c else TILE
                mm(bank(4 + qs % 2, w), NQ[0:SC, (BT * j + qs) * P:(BT * j + qs + 1) * P],
                   NK[0:SC, c * TILE:c * TILE + w], start=True, stop=True).then_inc(mx_ps, 1)

            transposes(XN, xn_rdy, seq_f(0), seq_f(0))
            pe.wait_ge(mix_v, 3 * HB)
            for i in range(4):
                for k in range(4):
                    last = nc.tensor.transpose(bank(2 + i)[:, k * P:(k + 1) * P],
                                               T1[:, (i % 2) * 4 + k, (i // 2) * P:(i // 2 + 1) * P], ident[:, :])
                last.then_inc(mu_ps, 1)
            pe.wait_ge(mu_ev, 4)
            for t in range(NT + 1):
                late, soon = mx0_beside(t)
                if t < NT:
                    pe.wait_ge(xt_rdy, seq_f(t) + 1)
                    for b in range(H_AHEAD):
                        if t and b == H_AHEAD - 2:
                            transposes(XN2A, xn_rdy, seq_p(t - 1), seq_p(t - 1))
                        turn_free("h", t * HB + b)
                        up_block(b, bank(turn_bank("h", t * HB + b)), late[2 * b:2 * b + 1])
                        for item in late[2 * b + 1:2 * b + 2]:
                            maximum0(*item)
                else:
                    for item in late:
                        maximum0(*item)
                    transposes(XN2A, xn_rdy, seq_p(t - 1), seq_p(t - 1))
                if t:
                    if t == 1:
                        pe.wait_ge(in_proj, 64)
                    pe.wait_ge(xt_rdy, seq_p(t - 1) + 1)
                    for w in range(4):
                        u = (t - 1) * 4 + w
                        turn_free("qk", u)
                        for k in range(DK):
                            last = mm(bank(turn_bank("qk", u)), (WQ if w < 2 else WK)[:, k, (w % 2) * P:(w % 2 + 1) * P],
                                      XT2A[:, k, :], start=(k == 0), stop=(k == DK - 1))
                        last.then_inc(qk_ps, 1)
                if t < NT:
                    for b in range(H_AHEAD, HB):
                        turn_free("h", t * HB + b)
                        up_block(b, bank(turn_bank("h", t * HB + b)))
                if t == 0:
                    fold_down()
                if t + 1 < NT:
                    transposes(XN, xn_rdy, seq_f(t + 1), seq_f(t + 1))
                if t:
                    for b in range(BT):
                        if b < 2:
                            pe.wait_ge(y_ev, (t - 1) * BT + b + 2 + 1 + FREE_Y)
                        else:
                            pe.wait_ge(v_ev, (t - 1) * BT + b + 1)
                        for k in range(DK):
                            last = mm(y_bank(b), XT2A[:, k, b * P:(b + 1) * P], WV[:, k, :],
                                      start=(k == 0), stop=(k == DK - 1))
                        last.then_inc(v_ps, 1)
                if t < NT:
                    pe.wait_ge(gelu_done, t * HB + HB + FREE_H)
                    if t == 0:
                        pe.wait_ge(md_ev, 4)
                    for b in range(BT):
                        if b < 2 and t:
                            pe.wait_ge(v_ev, (t - 1) * BT + b + 3 + FREE_V)
                        else:
                            pe.wait_ge(y_ev, t * BT + b + 1)
                        y_block(b, G, MD, HB, soon[BT * (b - 1):BT * b] if b else ())
            pe.wait_ge(rest_done, 4 * NT + FREE_QK)
            for seq in range(MX0_ALONE, NMX):
                n, qs = MX0_ALL[seq]
                if seq == MX0_START[NT - 1]:
                    pe.wait_ge(ld_nxt[NT - 1], SLICE)
                pe.wait_ge(mx_red, seq + 1)
                maximum(seq, n, qs)
            pe.wait_ge(v_ev, NT * BT + FREE_V)
            pe.wait_ge(att_init, 2)
            pe.wait_ge(const_rdy, 3)

            def scores(h, n, half):
                j, c = CH[n]
                if half == 0 and j == NT - 1:
                    pe.wait_ge(ld_cur[c], h * SLICE + SLICE)
                if half == 0 and n == 0:
                    pe.wait_ge(m_ld[0], h * 16 + 16)
                if half == 0 and n == LAST[4] + 1:
                    pe.wait_ge(m_ld[1], h * 16 + 16)
                q0 = 2 * P if (j == c and half and j) else 0
                pe.wait_ge(exp_done[half], h * NCH + n + 1)
                for k in range(2):
                    kb = c * BT + 2 * half + k
                    last = mm(PS[:, (2 * half + k) * 512 + q0:(2 * half + k + 1) * 512], CK[0:SM, kb * P:(kb + 1) * P],
                              CQ[0:SM, j * TILE + q0:(j + 1) * TILE], start=True, stop=True)
                last.then_inc(st_ps[half], 1)

            def values(h, n, part):
                j, c = CH[n]
                if j == c:
                    q = h * NT + (NT - 1 - j)
                    if part == 0 and not (isinstance(h, int) and h == 0 and n == 0):
                        pe.wait_ge(o_ev, q - 1 + FREE_O)
                    if part == 0 and j == 6:
                        pe.wait_ge(mt_ev, 2 * h + 2)
                    if part == 0 and j == 2 and not (isinstance(h, int) and h == H - 1):
                        pe.wait_ge(mt_ev, 2 * h + 3)
                    for half in (range(2) if j == 0 else (part,)):
                        pe.wait_ge(masked[half], 2 * q + 2)
                elif part == 0:
                    pe.wait_ge(exp_done[1], h * NCH + n + 2)
                if n < NT and part == 0:
                    pe.wait_ge(vh_rdy, h * NT + n + 1)
                for kb in range(BT):
                    first = kb * P if (j == c and j) else 0
                    q0, q1 = max(first, part * TILE // 2), (part + 1) * TILE // 2
                    if q0 < q1:
                        last = mm(o_bank(j, q0, q1 - q0)[kb * Q32:kb * Q32 + DV, :], VH[:, c * BT + kb, :],
                                  PB[n % 2][kb // 2][:, kb % 2, q0:q1], start=(j == c and q0 == first),
                                  stop=(c == 0), skip_group_check=True)
                if part:
                    last.then_inc(pv_done, 1)

            def add_tiles(h, j):
                q = h * NT + (NT - 1 - j)
                pe.wait_ge(ot_ev, q + 1)
                pe.wait_ge(o_ev, q + FREE_O)
                for b in range(BT):
                    last = mm(o_bank(j, 0, P)[b * Q32:(b + 1) * Q32, :], SEL[:, :], OTS[:, b * P:(b + 1) * P],
                              start=True, stop=True, skip_group_check=True)
                last.then_inc(os_ps, 1)

            def turn_sums(h, j):
                q = h * NT + (NT - 1 - j)
                pe.wait_ge(os_ev, q + 2)
                nc.tensor.transpose(o_bank(j, P, P), OS[:, :], ident[:, :]).then_inc(ot_ps, 1)

            def head_maximum(g, n, qs):
                j, c = CH[n]
                if qs == 0 and j == NT - 1:
                    pe.wait_ge(ld_nxt[c], g * SLICE + SLICE)
                pe.wait_ge(mx_red, g * NMX + n * BT + qs + 1)
                maximum(g * NMX + n * BT + qs, n, qs)

            def rows(i, grp, evacuated):
                if evacuated is not None:
                    pe.wait_ge(o_ev, evacuated)
                pe.wait_ge(m_rdy, i + 1)
                pe.sem_inc(passed[2], 1)
                nc.tensor.transpose(TURNED, MP[:, grp, :, :].rearrange("p a b -> p (a b)"), identb[:, :]).then_inc(mt_ps, 1)

            def turn(h, more):
                for s in range(LAG, NCH + LAG):
                    hs, n = slot(h, s)
                    ahead = s < NCH or more
                    done = chain(h, s)
                    if more:
                        head_maximum(h + 1, s - LAG, 0)
                    if ahead:
                        scores(hs, n, 0)
                    if more:
                        head_maximum(h + 1, s - LAG, 1)
                    if ahead:
                        scores(hs, n, 1)
                    for d in done:
                        add_tiles(*d)
                    if more:
                        head_maximum(h + 1, s - LAG, 2)
                    if s <= NCH or more:
                        values(*slot(h, s - 1), 0)
                    if more:
                        head_maximum(h + 1, s - LAG, 3)
                    for d in done:
                        turn_sums(*d)
                    if s <= NCH or more:
                        values(*slot(h, s - 1), 1)
                    if more and s == TA_AT:
                        rows(2 * h + 2, 0, h * NT + 4 + FREE_O)
                    if s == TB_AT:
                        rows(2 * h + 1, 1, h * NT + FREE_O)

            rows(0, 0, None)
            scores(0, 0, 0)
            scores(0, 0, 1)
            scores(0, 1, 0)
            scores(0, 1, 1)
            values(0, 0, 0)
            values(0, 0, 1)
            with pe.Fori(0, H - 1) as h:
                turn(h, True)
            turn(H - 1, False)

            def y_blocks(y, blocks, lhs, rhs, nk):
                for b in blocks:
                    pe.wait_ge(y_ev, y * BT + b + 1)
                    y_block(b, lhs, rhs, nk)

            def up2(t, ahead):
                pe.wait_ge(xt_rdy, seq_f2(t) + 1)
                for b in range(HB):
                    if b == 6 and ahead:
                        transposes(XN2B, or_rdy, t + 1, seq_w(t + 1))
                    pe.wait_ge(gelu_done, (t + NT) * HB + b + 1)
                    up_block(b, bank(2 + b % 4))

            transposes(XN2B, or_rdy, 0, seq_w(0))
            pe.wait_ge(xt_rdy, seq_w(0) + 1)
            y_blocks(Y_W0, range(BT), XT2B, WO, DK)
            transposes(XN, xn_rdy, 2 * NT, seq_f2(0))
            with pe.Fori(0, NT - 1) as t:
                up2(t, True)
                pe.wait_ge(xt_rdy, seq_w(t + 1) + 1)
                y_blocks(y_w(t + 1), range(BT), XT2B, WO, DK)
                pe.wait_ge(gelu_done, (t + NT) * HB + HB + FREE_H)
                y_blocks(y_f2(t), range(BT - 1), G, MD, HB)
                transposes(XN, xn_rdy, t + 2 * NT + 1, seq_f2(t + 1))
                y_blocks(y_f2(t), range(BT - 1, BT), G, MD, HB)
            up2(NT - 1, False)
            pe.wait_ge(gelu_done, 2 * NT * HB + FREE_H)
            y_blocks(Y_LAST, range(BT), G, MD, HB)


def kernel(L0_attn_x, L0_attn_WQ, L0_attn_WK, L0_attn_WV, L0_attn_WO, L0_ffn_W_exp, L0_ffn_b_exp,
           L0_ffn_up_weights, L0_ffn_up_bias, L0_ffn_down_weights, L0_ffn_W_con, L0_ffn_b_con, L0_ffn_down_bias):
    import numpy as np
    import concourse.bacc as bacc
    from concourse.bass_utils import run_bass_kernel_spmd

    def heads_last(w):
        return np.asarray(w).transpose(2, 0, 1).reshape(D, H * DH)

    arrays = {
        "x": np.asarray(L0_attn_x).reshape(S, D),
        "w_exp_t": np.concatenate([np.asarray(L0_ffn_W_exp).T, np.asarray(L0_ffn_b_exp)[:, None]], axis=1),
        "up_w": np.asarray(L0_ffn_up_weights).reshape(STAGES, HID // 2, 4),
        "up_b": np.asarray(L0_ffn_up_bias).reshape(HB, P).T,
        "down_w": np.asarray(L0_ffn_down_weights).reshape(STAGES, HID // 2, 4),
        "w_con": L0_ffn_W_con,
        "b_con": L0_ffn_b_con,
        "down_b": L0_ffn_down_bias,
        "wq": heads_last(L0_attn_WQ),
        "wk": heads_last(L0_attn_WK),
        "wv": heads_last(L0_attn_WV),
        "wo": np.asarray(L0_attn_WO).transpose(0, 2, 1).reshape(H * DH, D),
    }
    arrays = {n: np.ascontiguousarray(a) for n, a in arrays.items()}
    nc = bacc.Bacc("TRN2", target_bir_lowering=False, num_devices=1)
    ins = [nc.dram_tensor(n, a.shape, f32, kind="ExternalInput").ap() for n, a in arrays.items()]
    out = nc.dram_tensor("out", (S, D), f32, kind="ExternalOutput").ap()
    program(nc, *ins, out)
    r = run_bass_kernel_spmd(nc, [arrays], core_ids=[0])
    return r.results[0]["out"].reshape(1, S, D)
```
